# Optimizing a Trainium2 kernel written in Bass

```python
import numpy as np
import jax
import jax.numpy as jnp

def _softmax(x, axis=-1):
    return jax.nn.softmax(x, axis=axis)

def _gelu(x):
    return jax.nn.gelu(x, approximate=True)

def _silu(x):
    return jax.nn.silu(x)

def _sigmoid(x):
    return jax.nn.sigmoid(x)

def _layernorm(x, axis=-1, eps=1e-05):
    m = jnp.mean(x, axis=axis, keepdims=True)
    v = jnp.var(x, axis=axis, keepdims=True)
    return (x - m) / jnp.sqrt(v + eps)

def _scatter_add(tgt, idx, src, axis=0):
    return tgt.at[idx].add(src)

def _segment_sum(src, seg, n):
    return jax.ops.segment_sum(src, seg, n)
kernel_name = 'mk_flamingo_gated_d1_seqx_r4_4a680b'

def setup_inputs(seed: int=0):
    np.random.seed(seed)
    _w = jnp.asarray

    def _rec_inputs():
        import jax
        import jax.numpy as jnp
        _rk = jax.random.key(seed)
        x = 7.22e-05 + 1 * jax.random.normal(jax.random.fold_in(_rk, 1), (16, 256, 256), jnp.float32)
        _lenS = 256 - jax.random.randint(jax.random.fold_in(_rk, 7), (16,), 0, max(1, 256 // 4) + 1, jnp.int32)
        _lenS2 = 256 - jax.random.randint(jax.random.fold_in(_rk, 8), (16,), 0, max(1, 256 // 4) + 1, jnp.int32)
        _ctx_1024P = jax.random.normal(jax.random.fold_in(_rk, 11), (16, 16, 256), jnp.float32)
        _ctx_1024c = jax.random.dirichlet(jax.random.fold_in(_rk, 511), 0.3 * jnp.ones((16,), jnp.float32), (16, 256))
        _ctx_1024t = jnp.einsum('bsk,bkd->bsd', _ctx_1024c, _ctx_1024P)
        _ctx_1024t = _ctx_1024t * jax.lax.rsqrt(jnp.mean(jnp.square(_ctx_1024t)) + 1e-12) * 0.953939
        ctx_1024 = 4.13588e-05 + 0.999923 * (_ctx_1024t + 0.3 * jax.random.normal(jax.random.fold_in(_rk, 611), (16, 256, 256), jnp.float32))
        _g = jax.random.normal(jax.random.fold_in(_rk, 9001), (2, 1), jnp.float32)
        _g = jnp.sign(_g) * jnp.maximum(jnp.abs(_g), 1.0) + (_g == 0) * 1.0
        g_xattn = _g[0]
        g_ffn = _g[1]
        return (x, ctx_1024, g_xattn, g_ffn)
    x, ctx_1024, g_xattn, g_ffn = _rec_inputs()

    def _L0_xattn_setup():
        import jax, jax.numpy as jnp
        import numpy as np
        EMBED_DIM = 256
        NUM_HEADS = 16
        HEAD_DIM = EMBED_DIM // NUM_HEADS
        key = jax.random.key(seed)
        ks = jax.random.split(key, 11)
        B, S, D = (4, 512, EMBED_DIM)
        scale = 1.0 / np.sqrt(D)
        inp = {'Q': jax.random.normal(ks[0], (B, S, D), jnp.float32), 'K': jax.random.normal(ks[1], (B, S, D), jnp.float32), 'V': jax.random.normal(ks[2], (B, S, D), jnp.float32), 'Wq': jax.random.normal(ks[3], (D, D), jnp.float32) * scale, 'bq': jax.random.normal(ks[4], (D,), jnp.float32) * 0.01, 'Wk': jax.random.normal(ks[5], (D, D), jnp.float32) * scale, 'bk': jax.random.normal(ks[6], (D,), jnp.float32) * 0.01, 'Wv': jax.random.normal(ks[7], (D, D), jnp.float32) * scale, 'bv': jax.random.normal(ks[8], (D,), jnp.float32) * 0.01, 'Wo': jax.random.normal(ks[9], (D, D), jnp.float32) * scale, 'bo': jax.random.normal(ks[10], (D,), jnp.float32) * 0.01}
        return inp
    _L0_xattn_all = _L0_xattn_setup()
    _L0_xattn_in = {k: v for k, v in _L0_xattn_all.items() if k in ('Wq', 'bq', 'Wk', 'bk', 'Wv', 'bv', 'Wo', 'bo')}
    del _L0_xattn_all

    def _L0_ffn_setup():
        import jax, jax.numpy as jnp
        import numpy as np
        BLOCK = 32
        W_BITS = 4
        ACT_BITS = 16

        def act_qdq(x):
            qmax = 2.0 ** (ACT_BITS - 1) - 1.0
            scale = jnp.maximum(jnp.max(jnp.abs(x)) / qmax, 1e-12)
            return jnp.clip(jnp.round(x / scale), -qmax - 1.0, qmax) * scale

        def fixed_qdq_u16(x):
            scale = 1.0 / 65536.0
            return jnp.clip(jnp.round(x / scale), 0.0, 65535.0) * scale

        def lpbq_dequant(w):
            O, I = w.shape
            qmax = 2.0 ** (W_BITS - 1) - 1.0
            wb = w.reshape(O, I // BLOCK, BLOCK)
            s = jnp.maximum(jnp.max(jnp.abs(wb), axis=-1, keepdims=True) / qmax, 1e-12)
            wq = jnp.clip(jnp.round(wb / s), -qmax - 1.0, qmax) * s
            return wq.reshape(O, I)
        key = jax.random.key(seed)
        k1, k2, k3, k4 = jax.random.split(key, 4)
        B, S, H, I = (2, 1024, 256, 768)
        x = jax.random.normal(k1, (B, S, H), jnp.float32)
        w_gate = jax.random.normal(k2, (I, H), jnp.float32) * 0.02
        w_up = jax.random.normal(k3, (I, H), jnp.float32) * 0.02
        w_down = jax.random.normal(k4, (H, I), jnp.float32) * 0.02
        return {'x': x, 'w_gate': w_gate, 'w_up': w_up, 'w_down': w_down}
    _L0_ffn_all = _L0_ffn_setup()
    _L0_ffn_in = {k: v for k, v in _L0_ffn_all.items() if k in ('w_gate', 'w_up', 'w_down')}
    del _L0_ffn_all
    return {'x': x, 'ctx_1024': ctx_1024, 'g_xattn': g_xattn, 'g_ffn': g_ffn, 'L0_xattn_Wq': _L0_xattn_in['Wq'], 'L0_xattn_bq': _L0_xattn_in['bq'], 'L0_xattn_Wk': _L0_xattn_in['Wk'], 'L0_xattn_bk': _L0_xattn_in['bk'], 'L0_xattn_Wv': _L0_xattn_in['Wv'], 'L0_xattn_bv': _L0_xattn_in['bv'], 'L0_xattn_Wo': _L0_xattn_in['Wo'], 'L0_xattn_bo': _L0_xattn_in['bo'], 'L0_ffn_w_gate': _L0_ffn_in['w_gate'], 'L0_ffn_w_up': _L0_ffn_in['w_up'], 'L0_ffn_w_down': _L0_ffn_in['w_down']}

def reference(x, ctx_1024, g_xattn, g_ffn, L0_xattn_Wq, L0_xattn_bq, L0_xattn_Wk, L0_xattn_bk, L0_xattn_Wv, L0_xattn_bv, L0_xattn_Wo, L0_xattn_bo, L0_ffn_w_gate, L0_ffn_w_up, L0_ffn_w_down):
    import jax
    import jax.numpy as jnp

    def _L0_xattn_ref(Q, K, V, Wq, bq, Wk, bk, Wv, bv, Wo, bo):
        import jax, jax.numpy as jnp
        import numpy as np
        EMBED_DIM = 256
        NUM_HEADS = 16
        HEAD_DIM = EMBED_DIM // NUM_HEADS
        B, S, D = Q.shape
        H, Hd = (NUM_HEADS, HEAD_DIM)
        q = Q @ Wq.T + bq
        k = K @ Wk.T + bk
        v = V @ Wv.T + bv
        q = q.reshape(B, S, H, Hd).transpose(0, 2, 1, 3)
        k = k.reshape(B, S, H, Hd).transpose(0, 2, 1, 3)
        v = v.reshape(B, S, H, Hd).transpose(0, 2, 1, 3)
        scores = jnp.einsum('bhqd,bhkd->bhqk', q, k) / jnp.sqrt(jnp.float32(Hd))
        attn = jax.nn.softmax(scores, axis=-1)
        out = jnp.einsum('bhqk,bhkd->bhqd', attn, v)
        out = out.transpose(0, 2, 1, 3).reshape(B, S, D)
        return out @ Wo.T + bo

    def _L0_ffn_ref(x, w_gate, w_up, w_down):
        import jax, jax.numpy as jnp
        import numpy as np
        BLOCK = 32
        W_BITS = 4
        ACT_BITS = 16

        def act_qdq(x):
            qmax = 2.0 ** (ACT_BITS - 1) - 1.0
            scale = jnp.maximum(jnp.max(jnp.abs(x)) / qmax, 1e-12)
            return jnp.clip(jnp.round(x / scale), -qmax - 1.0, qmax) * scale

        def fixed_qdq_u16(x):
            scale = 1.0 / 65536.0
            return jnp.clip(jnp.round(x / scale), 0.0, 65535.0) * scale

        def lpbq_dequant(w):
            O, I = w.shape
            qmax = 2.0 ** (W_BITS - 1) - 1.0
            wb = w.reshape(O, I // BLOCK, BLOCK)
            s = jnp.maximum(jnp.max(jnp.abs(wb), axis=-1, keepdims=True) / qmax, 1e-12)
            wq = jnp.clip(jnp.round(wb / s), -qmax - 1.0, qmax) * s
            return wq.reshape(O, I)
        x = act_qdq(x)
        up = act_qdq(x @ lpbq_dequant(w_up).T)
        gate = act_qdq(x @ lpbq_dequant(w_gate).T)
        sig = fixed_qdq_u16(jax.nn.sigmoid(gate))
        gate = act_qdq(gate * sig)
        o = act_qdq(gate * up)
        return o @ lpbq_dequant(w_down).T
    x = x + jnp.tanh(g_xattn[0]) * _L0_xattn_ref(_layernorm(x, axis=-1), ctx_1024, ctx_1024, L0_xattn_Wq, L0_xattn_bq, L0_xattn_Wk, L0_xattn_bk, L0_xattn_Wv, L0_xattn_bv, L0_xattn_Wo, L0_xattn_bo)
    x = x + jnp.tanh(g_ffn[0]) * _L0_ffn_ref(_layernorm(x, axis=-1), L0_ffn_w_gate, L0_ffn_w_up, L0_ffn_w_down)
    return x

_drawn_inputs = setup_inputs


def setup_inputs(seed=0):
    import zlib

    import numpy as np

    out = dict(_drawn_inputs(seed))
    spreads = {}
    factors = {'L0_xattn_bq': 35.621, 'L0_xattn_bk': 64.0, 'L0_xattn_bv': 8.0, 'L0_xattn_bo': 7.816}
    for name, (base, spread) in spreads.items():
        noise = np.random.default_rng([zlib.crc32(name.encode()), seed]).standard_normal(out[name].shape)
        drawn = base * np.exp(spread * noise) if base else spread * noise
        out[name] = jnp.asarray(drawn.astype(out[name].dtype))
    for name, factor in factors.items():
        out[name] = (out[name] * factor).astype(out[name].dtype)
    return out
```

```python
from contextlib import ExitStack

import concourse.bass as bass
from concourse import mybir

ALU = mybir.AluOpType
ACT = mybir.ActivationFunctionType
AX = mybir.AxisListType
F32 = mybir.dt.float32
F16 = mybir.dt.float16
I16 = mybir.dt.int16
U16 = mybir.dt.uint16
RMAX = bass.bass_isa.ReduceOp.absmax

P = 128
EPS = 1e-5
WS = 16.0
FS = 256.0
MS = 64.0
HD = 16
NH = 16
PAIRS = NH // 2
QMAX = 32767.0
LEVELS = 65536.0


def attention(nc, t, x, ctx, out):
    NB, S, D = x.shape
    KT = S // P
    SPAN = range(-3, NB + 2)
    FIRST = 4
    LAST = FIRST + 3 * ((NB - 3 - FIRST) // 3) - 1

    xv = x.rearrange("b (p t) d -> b p t d", t=KT)
    cv = ctx.rearrange("b (p t) d -> b p t d", t=KT)
    ov = out.rearrange("b (p t) d -> b p t d", t=KT)

    qk_dram = nc.dram_tensor("qk_dram", (3, 4, 2, HD, 4 * KT * S), F16, kind="Internal").ap()
    rec_dram = nc.dram_tensor("rec_dram", (3, 4, 4 * S), F32, kind="Internal").ap()

    with ExitStack() as es:
        def sb(name, shape, dt):
            return es.enter_context(nc.sbuf_tensor(name, shape, dt))

        def pb(name, shape, dt):
            return es.enter_context(nc.psum_tensor(name, shape, dt))

        def sem(name):
            return es.enter_context(nc.semaphore(name))

        ident = sb("ident", [P, P], F32)
        wf = {n: sb("wf_" + n, [P, 2, D], F32) for n in "qkv"}
        wh = {n: sb("wh_" + n, [P, 2, D], F16) for n in "qkv"}
        wl = {n: sb("wl_" + n, [P, 2, D], F16) for n in "qkv"}
        wof = sb("wof", [P, 4, D], F32)
        woh = sb("woh", [P, 4, D], F16)
        wol = sb("wol", [P, 4, D], F16)
        bqk = sb("bqk", [P, 2, 2], F32)
        bqk_s = sb("bqk_s", [P, 2, 2], F32)
        bv = sb("bv", [P, D], F32)
        bo = sb("bo", [P, D], F32)
        tbo = sb("tbo", [P, D], F32)
        gx = sb("gx", [P, 1], F32)
        tg = sb("tg", [P, 1], F32)
        tgs = sb("tgs", [P, 1], F32)
        half = sb("half", [P, KT], F32)

        xt = sb("xt", [P, 3, KT, D], F32)
        ct = sb("ct", [P, KT, D], F32)
        xn = sb("xn", [P, KT, D], F32)
        stats = sb("stats", [P, KT, 6], F32)
        mv = sb("mv", [P, KT, 2], F32)
        ve = sb("ve", [P, KT], F32)
        rstd = sb("rstd", [P, KT], F32)
        xh = sb("xh", [P, 2, S], F16)
        xl = sb("xl", [P, 2, S], F16)
        ch = sb("ch", [P, 2, S], F16)
        cl = sb("cl", [P, 2, S], F16)
        qk = sb("qk", [P, 4, 2, S], F16)
        kst = sb("kst", [97, 3, PAIRS, S], F16)
        qst = sb("qst", [97, 3, 2, PAIRS, S], F16)
        vt = sb("vt", [P, 3, KT, NH, 32], F32)
        negm = sb("negm", [P, 3, KT, NH], F32)
        mrow = sb("mrow", [8, 2, S], F16)
        pt = sb("pt", [P, 2, 2, KT, 2, S], F32)
        ot = sb("ot", [P, 3, 4, S], F32)
        den = sb("den", [P, 32], F32)
        rec = sb("rec", [P, 32], F32)
        recb = sb("recb", [P, 4, S], F32)
        at = sb("at", [P, 4, S], F32)
        ah = sb("ah", [P, 4, S], F16)
        al = sb("al", [P, 4, S], F16)
        xr = sb("xr", [P, KT, D], F32)
        xb = sb("xb", [P, KT, D], F32)
        y = sb("y", [P, KT, D], F32)
        stats2 = sb("stats2", [P, KT, 6], F32)
        mv2 = sb("mv2", [P, KT, 2], F32)
        ve2 = sb("ve2", [P, KT], F32)
        rstd2 = sb("rstd2", [P, KT], F32)
        ln = sb("ln", [P, KT, D], F32)
        lmax = sb("lmax", [P, 1], F32)

        s_ps = [pb(f"s_ps{i}", [P, 2, S], F32) for i in range(2)]
        st_ps = [pb(f"st_ps{i}", [P, KT, 2, S], F32) for i in range(2)]
        pv_ps = pb("pv_ps", [P, 2, S], F32)
        misc = pb("misc", [P, 2, S], F32)

        ident_set = sem("ident_set")
        consts_set = sem("consts_set")
        w_loaded = sem("w_loaded")
        wo_loaded = sem("wo_loaded")
        b_loaded = sem("b_loaded")
        g_loaded = sem("g_loaded")
        wo_zeroed = sem("wo_zeroed")
        weights_split = sem("weights_split")
        gate_done = sem("gate_done")
        gate_scaled = sem("gate_scaled")
        bias_ready = sem("bias_ready")
        x_loaded = sem("x_loaded")
        c_loaded = sem("c_loaded")
        stats_done = sem("stats_done")
        mv_done = sem("mv_done")
        ve_done = sem("ve_done")
        rstd_done = sem("rstd_done")
        xn_ready = sem("xn_ready")
        xt_done = sem("xt_done")
        xh_done = sem("xh_done")
        xl_done = sem("xl_done")
        ct_done = sem("ct_done")
        ch_done = sem("ch_done")
        cl_done = sem("cl_done")
        q_done = sem("q_done")
        qh_done = sem("qh_done")
        ql_done = sem("ql_done")
        k_done = sem("k_done")
        kh_done = sem("kh_done")
        kl_done = sem("kl_done")
        q_written = sem("q_written")
        k_written = sem("k_written")
        stack_loaded = sem("stack_loaded")
        s_done = sem("s_done")
        max_done = sem("max_done")
        mt_done = sem("mt_done")
        mh_done = sem("mh_done")
        ma_loaded = sem("ma_loaded")
        mb_loaded = sem("mb_loaded")
        st_done = sem("st_done")
        exp_done = sem("exp_done")
        v_done = sem("v_done")
        v_taken = sem("v_taken")
        pv_done = sem("pv_done")
        ot_taken = sem("ot_taken")
        den_loaded = sem("den_loaded")
        rec_done = sem("rec_done")
        rec_written = sem("rec_written")
        rec_loaded = sem("rec_loaded")
        at_done = sem("at_done")
        ah_done = sem("ah_done")
        al_done = sem("al_done")
        xr_loaded = sem("xr_loaded")
        xb_done = sem("xb_done")
        o_done = sem("o_done")
        y_done = sem("y_done")
        y_stored = sem("y_stored")
        stats2_done = sem("stats2_done")
        mv2_done = sem("mv2_done")
        ve2_done = sem("ve2_done")
        rstd2_done = sem("rstd2_done")
        ln_done = sem("ln_done")
        ln_stored = sem("ln_stored")
        lmax_tmp = sem("lmax_tmp")
        lmax_done = sem("lmax_done")
        counts = {e.engine: e.alloc_register("count") for e in (nc.gpsimd, nc.sync, nc.scalar, nc.vector)}

        def count(n):
            return max(n, 0) if isinstance(n, int) else n

        def held(eng, n):
            if isinstance(n, int):
                return max(n, 0)
            eng.reg_mov(counts[eng.engine], n)
            eng.wait_ge(ident_set, 1)
            return counts[eng.engine]

        def upto(it, k):
            return min(max(it + k + 1, 0), NB) if isinstance(it, int) else it + (k + 1)

        def has(it, k):
            return not isinstance(it, int) or 0 <= it + k < NB

        def iterations(eng, body):
            for it in SPAN:
                if it < FIRST:
                    body(it, it % 3)
            with eng.Fori(FIRST, LAST - 1, 3) as i:
                for d in range(3):
                    body(i + d, (FIRST + d) % 3)
            for it in SPAN:
                if it > LAST:
                    body(it, it % 3)

        block = es.enter_context(nc.Block())

        @block.sync
        def _(sp):
            for n in "qkv":
                sp.dma_start(wf[n][:], t["w" + n].rearrange("(t p) e -> p t e", p=P)).then_inc(w_loaded, 16)
            sp.dma_start(bqk[:, 0, :], t["bq"]).then_inc(b_loaded, 16)
            sp.dma_start(bqk[:, 1, :], t["bk"]).then_inc(b_loaded, 16)
            sp.dma_start(bv[:], t["bv"].rearrange("(o d) -> o d", o=1).broadcast_to((P, D))).then_inc(b_loaded, 16)
            sp.dma_start(bo[:], t["bo"].rearrange("(o d) -> o d", o=1).broadcast_to((P, D))).then_inc(b_loaded, 16)
            sp.dma_start(gx[:], t["gx"].rearrange("(o d) -> o d", o=1).broadcast_to((P, 1))).then_inc(g_loaded, 16)
            sp.wait_ge(wo_zeroed, 1)
            for c in range(4):
                h0 = 8 * (c // 2) + c % 2
                src = t["wo"].rearrange("(h j) n -> j h n", j=HD)[:, h0:h0 + 7:2, :]
                sp.dma_start(wof[32 * c:32 * c + HD, :, :], src).then_inc(wo_loaded, 16)
            sp.wait_ge(consts_set, 4)

            def body(it, b):
                n = (b + 2) % 3
                if has(it, -2):
                    sp.wait_ge(y_done, held(sp, upto(it, -2)))
                    sp.dma_start(ov[it - 2], y[:]).then_inc(y_stored, 16)
                if has(it, -1):
                    sp.wait_ge(xb_done, held(sp, upto(it, -2)))
                    sp.dma_start(xr[:], xv[it - 1]).then_inc(xr_loaded, 16)
                if has(it, 3):
                    sp.wait_ge(xn_ready, held(sp, upto(it, 0)))
                    sp.wait_ge(x_loaded, held(sp, 16 * upto(it, 2)))
                    sp.dma_start(xt[:, b], xv[it + 3]).then_inc(x_loaded, 16)
                if has(it, -1):
                    sp.wait_ge(ot_taken, held(sp, 2 * upto(it, -1)))
                    sp.wait_ge(rec_done, held(sp, upto(it, -2)))
                    sp.dma_start(den[:], ot[HD:P:32, n].rearrange("p u q -> p (u q)")).then_inc(den_loaded, 16)
                if has(it, 0):
                    sp.wait_ge(mh_done, held(sp, 2 * it + 2))
                    for r in range(2):
                        sp.dma_start(qst[96:97, b, r, 4:8, :], mrow[4 * r:4 * r + 4, 1, :]).then_inc(mb_loaded, 16)
                if has(it, -1):
                    sp.wait_ge(rec_done, held(sp, upto(it, -1)))
                    sp.dma_start(rec_dram[n].rearrange("c (g w) -> (c g) w", w=32), rec[:]).then_inc(rec_written, 16)
                if has(it, -2):
                    sp.wait_ge(ln_done, held(sp, KT * upto(it, -2)))
                    sp.dma_start(t["lnall"][:, it - 2, :], ln[:].rearrange("p t d -> p (t d)")).then_inc(ln_stored, 16)
                if has(it, 3):
                    sp.wait_ge(ct_done, held(sp, upto(it, 2)))
                    sp.dma_start(ct[:], cv[it + 3]).then_inc(c_loaded, 16)
                if has(it, -1):
                    sp.wait_ge(rec_written, held(sp, 16 * upto(it, -1)))
                    sp.wait_ge(at_done, held(sp, upto(it, -2)))
                    sp.dma_start(recb[:].rearrange("p u q -> p (u q)"),
                                 rec_dram[n].rearrange("c (o w) -> c o w", o=1).broadcast_to((4, 32, 4 * S))
                                 ).then_inc(rec_loaded, 16)
                kd = kst[:, n].rearrange("p j q -> p (j q)")
                qd = [qst[:, n, r].rearrange("p j q -> p (j q)") for r in range(2)]
                if has(it, 2):
                    sp.wait_ge(stack_loaded, held(sp, 128 * upto(it, -1)))
                    for i, (ready, written) in enumerate(((qh_done, q_written), (ql_done, q_written), (kh_done, k_written), (kl_done, k_written))):
                        sp.wait_ge(ready, held(sp, upto(it, 2)))
                        sp.dma_start(qk_dram[n, i].rearrange("r j (a c) -> a (r j) c", a=4),
                                     qk[:, i].rearrange("p t q -> p (t q)")).then_inc(written, 16)
                    sp.wait_ge(st_done, held(sp, PAIRS * upto(it, -1)))
                    sp.wait_ge(q_written, held(sp, 32 * upto(it, 2)))
                    for r in range(2):
                        lo = 48 * r
                        sp.dma_start(qd[r][lo:lo + 2 * HD], qk_dram[n, 0:1, r].broadcast_to((2, HD, 4 * KT * S))
                                     ).then_inc(stack_loaded, 16)
                        sp.dma_start(qd[r][lo + 2 * HD:lo + 3 * HD], qk_dram[n, 1, r]).then_inc(stack_loaded, 16)
                if has(it, 1):
                    sp.wait_ge(mh_done, held(sp, 2 * it + 3))
                    for r in range(2):
                        sp.dma_start(qst[96:97, (b + 1) % 3, r, 0:4, :], mrow[4 * r:4 * r + 4, 0, :]).then_inc(ma_loaded, 16)
                if has(it, 2):
                    sp.wait_ge(k_written, held(sp, 32 * upto(it, 2)))
                    for r in range(2):
                        lo = 48 * r
                        sp.dma_start(kd[lo:lo + 2 * HD], qk_dram[n, 2:4, r]).then_inc(stack_loaded, 16)
                        sp.dma_start(kd[lo + 2 * HD:lo + 3 * HD], qk_dram[n, 2, r]).then_inc(stack_loaded, 16)

            iterations(nc.sync, body)
            sp.wait_ge(y_stored, 16 * NB)
            sp.wait_ge(ln_stored, 16 * NB)

        @block.tensor
        def _(pe):
            def split_product(o, lh, ll, rh, rl, last):
                terms = [(l, r, k) for l, r in ((lh, rh), (lh, rl), (ll, rh)) for k in range(last)]
                for n, (l, r, k) in enumerate(terms):
                    mm = nc.tensor.matmul(o, l(k), r(k), start=n == 0, stop=n == len(terms) - 1)
                return mm

            def project(nm, xh_, xl_, done):
                for e in range(2):
                    mm = split_product(misc[:, e, :], lambda k: wh[nm][:, k, e * P:(e + 1) * P],
                                       lambda k: wl[nm][:, k, e * P:(e + 1) * P],
                                       lambda k: xh_[:, k, :], lambda k: xl_[:, k, :], 2)
                mm.then_inc(done, 1)

            def turn(src, done):
                for d in range(2):
                    for tt in range(KT):
                        mm = nc.tensor.transpose(misc[:, d, tt * P:(tt + 1) * P], src[:, tt, d * P:(d + 1) * P], ident[:])
                mm.then_inc(done, 1)

            def turn_max(b, hf):
                for tt in range(KT):
                    mm = nc.tensor.transpose(misc[0:8, 0, tt * P:(tt + 1) * P],
                                             negm[:, b, tt, 8 * hf:8 * hf + 8], ident[:])
                mm.then_inc(mt_done, 1)

            def values(bat, b, u):
                pe.wait_ge(exp_done, count(PAIRS * bat + 2 * u + 2))
                if u % 2 == 0:
                    pe.wait_ge(ot_taken, count(2 * bat + u // 2))
                for kt in range(KT):
                    for c in range(4):
                        mm = nc.tensor.matmul(pv_ps[32 * c:32 * c + 32, u % 2, :],
                                              vt[:, b, kt, 8 * (c // 2) + 2 * u + c % 2, :],
                                              pt[:, u % 2, c // 2, kt, c % 2, :],
                                              start=kt == 0, stop=kt == KT - 1)
                mm.then_inc(pv_done, 1)

            pe.wait_ge(ident_set, 2)
            pe.wait_ge(weights_split, 8)
            pe.wait_ge(consts_set, 4)

            def body(it, b):
                for j in range(PAIRS):
                    if j == 0 and has(it, 2):
                        pe.wait_ge(v_taken, upto(it, 1))
                        pe.wait_ge(y_done, upto(it, -2))
                        pe.wait_ge(xn_ready, upto(it, 2))
                        turn(xn, xt_done)
                    if j == 1 and has(it, 0):
                        pe.wait_ge(y_done, upto(it, -2))
                        pe.wait_ge(xl_done, upto(it, 2))
                        pe.wait_ge(max_done, 16 * upto(it, 0))
                        turn_max(b, 1)
                    if j == 2 and has(it, 2):
                        pe.wait_ge(xl_done, upto(it, 2))
                        pe.wait_ge(mh_done, 2 * upto(it, 0))
                        pe.wait_ge(c_loaded, 16 * upto(it, 2))
                        turn(ct, ct_done)
                    if j == 3 and has(it, 2):
                        pe.wait_ge(cl_done, upto(it, 2))
                        project("q", xh, xl, q_done)
                    if j == 4 and has(it, 2):
                        pe.wait_ge(ql_done, upto(it, 2))
                        pe.wait_ge(qh_done, upto(it, 2))
                        project("k", ch, cl, k_done)
                    if j == 5 and has(it, 1):
                        pe.wait_ge(kl_done, upto(it, 2))
                        pe.wait_ge(kh_done, upto(it, 2))
                        pe.wait_ge(mh_done, 2 * upto(it, 0))
                        pe.wait_ge(max_done, count(16 * (it + 1) + 8))
                        turn_max((b + 1) % 3, 0)
                    if j == 6 and has(it, 2):
                        pe.wait_ge(kl_done, upto(it, 2))
                        pe.wait_ge(kh_done, upto(it, 2))
                        if has(it, 1):
                            pe.wait_ge(mh_done, count(2 * it + 3))
                        for tt in range(KT):
                            mm = split_product(misc[:, tt, :], lambda k: ch[:, k, tt * P:(tt + 1) * P],
                                               lambda k: cl[:, k, tt * P:(tt + 1) * P],
                                               lambda k: wh["v"][:, k, :], lambda k: wl["v"][:, k, :], 2)
                        mm.then_inc(v_done, 1)
                    if j == 7 and has(it, -1):
                        pe.wait_ge(v_taken, upto(it, 2))
                        pe.wait_ge(mh_done, 2 * upto(it, 0))
                        pe.wait_ge(y_done, upto(it, -2))
                        pe.wait_ge(al_done, upto(it, -1))
                        pe.wait_ge(ah_done, upto(it, -1))
                        for tt in range(KT):
                            mm = split_product(misc[:, tt, :], lambda k: ah[:, k, tt * P:(tt + 1) * P],
                                               lambda k: al[:, k, tt * P:(tt + 1) * P],
                                               lambda k: woh[:, k, :], lambda k: wol[:, k, :], 4)
                        mm.then_inc(o_done, 1)

                    if has(it, 1):
                        n = (b + 1) % 3
                        if j == 0:
                            pe.wait_ge(stack_loaded, 128 * upto(it, 1))
                        for tt in range(KT):
                            pe.wait_ge(max_done, count(16 * (it + 1) + 2 * j + tt - 1))
                            for r in range(2):
                                mm = nc.tensor.matmul(s_ps[tt][:, r, :], qst[0:96, n, r, j, tt * P:(tt + 1) * P],
                                                      kst[0:96, n, j, :], start=True, stop=True)
                            mm.then_inc(s_done, 1)
                    if has(it, 0):
                        if j == 0:
                            pe.wait_ge(ma_loaded, count(32 * it + 32))
                        if j == 4:
                            pe.wait_ge(mb_loaded, count(32 * it + 32))
                        pe.wait_ge(exp_done, count(PAIRS * it + j - 1))
                        for kt in range(KT):
                            mm = nc.tensor.matmul(st_ps[j % 2][:, kt], kst[:, b, j, kt * P:(kt + 1) * P],
                                                  qst[:, b, :, j, :], start=True, stop=True)
                        mm.then_inc(st_done, 1)
                    if j == 0 and has(it, -1):
                        values(it - 1, (b + 2) % 3, 3)
                    if j in (2, 4, 6) and has(it, 0):
                        if j == 2:
                            pe.wait_ge(v_taken, count(it + 1))
                        values(it, b, j // 2 - 1)

            iterations(nc.tensor, body)

        @block.scalar
        def _(act):
            act.wait_ge(g_loaded, 16)
            nc.scalar.activation(tg[:], gx[:], ACT.Tanh).then_inc(gate_done, 1)
            act.wait_ge(w_loaded, 48)
            for n in "qkv":
                nc.scalar.activation(wh[n][:], wf[n][:], ACT.Copy, scale=WS).then_inc(weights_split, 1)
            act.wait_ge(wo_loaded, 64)
            nc.scalar.activation(woh[:], wof[:], ACT.Copy, scale=WS).then_inc(weights_split, 1)
            act.wait_ge(bias_ready, 1)

            def take(bat, b, hf):
                act.wait_ge(pv_done, count(4 * bat + 2 * hf + 2))
                act.wait_ge(at_done, count(bat - 2))
                nc.scalar.copy(ot[:, b, 2 * hf:2 * hf + 2, :], pv_ps[:]).then_inc(ot_taken, 1)

            def max_row(bat, hf):
                act.wait_ge(mt_done, count(2 * bat + hf + 1))
                act.wait_ge((ma_loaded, mb_loaded)[hf], count(32 * bat))
                nc.scalar.activation(mrow[:, hf, :], misc[0:8, 0, :], ACT.Copy, scale=1.0 / MS).then_inc(mh_done, 1)

            def high(i, done):
                for e in range(2):
                    op = nc.scalar.activation(qk[:, 2 * i, e, :], misc[:, e, :], ACT.Identity, bias=bqk_s[:, i, e:e + 1])
                op.then_inc(done, 1)

            def body(it, b):
                for j in range(PAIRS):
                    if j == 0 and has(it, 2):
                        act.wait_ge(xt_done, upto(it, 2))
                        act.wait_ge(q_done, upto(it, 1))
                        nc.scalar.copy(xh[:], misc[:]).then_inc(xh_done, 1)
                    if j == 1 and has(it, 0):
                        max_row(it, 1)
                    if j == 2 and has(it, 2):
                        act.wait_ge(ct_done, upto(it, 2))
                        act.wait_ge(v_done, upto(it, 1))
                        nc.scalar.copy(ch[:], misc[:]).then_inc(ch_done, 1)
                    if j == 3 and has(it, 2):
                        act.wait_ge(q_done, upto(it, 2))
                        act.wait_ge(q_written, 32 * upto(it, 1))
                        high(0, qh_done)
                    if j == 4 and has(it, 2):
                        act.wait_ge(k_done, upto(it, 2))
                        act.wait_ge(k_written, 32 * upto(it, 1))
                        high(1, kh_done)
                    if j == 5 and has(it, 1):
                        max_row(it + 1, 0)
                    if j == 6 and has(it, -1):
                        act.wait_ge(at_done, upto(it, -1))
                        act.wait_ge(o_done, upto(it, -2))
                        nc.scalar.copy(ah[:], at[:]).then_inc(ah_done, 1)
                    if has(it, 0):
                        act.wait_ge(st_done, count(PAIRS * it + j + 1))
                        act.wait_ge(pv_done, count(4 * it + j // 2 - 1))
                        nc.scalar.activation(pt[:, (j // 2) % 2, j % 2], st_ps[j % 2][:], ACT.Exp,
                                             scale=1.0 / (WS * WS * HD ** 0.5)).then_inc(exp_done, 1)
                    if j == 0 and has(it, -1):
                        take(it - 1, (b + 2) % 3, 1)
                    if j == 4 and has(it, 0):
                        take(it, b, 0)

            iterations(nc.scalar, body)

        @block.vector
        def _(dve):
            nc.vector.memset(half[:], -0.5).then_inc(consts_set, 1)
            nc.vector.memset(lmax[:], 0.0).then_inc(lmax_done, 1)
            nc.vector.memset(wof[:], 0.0).then_inc(wo_zeroed, 1)
            nc.vector.memset(qst[:], 0.0).then_inc(consts_set, 1)
            nc.vector.memset(kst[96:97], MS).then_inc(consts_set, 1)
            dve.wait_ge(b_loaded, 64)
            nc.vector.tensor_scalar(bqk_s[:], bqk[:], WS, None, ALU.mult).then_inc(bias_ready, 1)
            dve.wait_ge(gate_done, 1)
            nc.vector.tensor_scalar(tgs[:], tg[:], 1.0 / WS, None, ALU.mult).then_inc(gate_scaled, 1)
            nc.vector.tensor_scalar(tbo[:], bo[:], tg[:, 0:1], None, ALU.mult).then_inc(gate_scaled, 1)
            dve.wait_ge(weights_split, 4)
            for n in "qkv":
                nc.vector.scalar_tensor_tensor(out=wl[n][:], in0=wf[n][:], scalar=WS, in1=wh[n][:], op0=ALU.mult,
                                               op1=ALU.subtract).then_inc(weights_split, 1)
            nc.vector.scalar_tensor_tensor(out=wol[:], in0=wof[:], scalar=WS, in1=woh[:], op0=ALU.mult,
                                           op1=ALU.subtract).then_inc(weights_split, 1)
            dve.wait_ge(gate_scaled, 2)
            dve.wait_ge(consts_set, 4)

            def low(i, done):
                for e in range(2):
                    op = nc.vector.scalar_tensor_tensor(out=qk[:, 2 * i + 1, e, :], in0=misc[:, e, :],
                                                        scalar=bqk_s[:, i, e:e + 1], in1=qk[:, 2 * i, e, :],
                                                        op0=ALU.add, op1=ALU.subtract)
                op.then_inc(done, 1)

            def body(it, b):
                for j in range(PAIRS):
                    if j == 0 and has(it, 2):
                        dve.wait_ge(xh_done, upto(it, 2))
                        nc.vector.tensor_tensor(xl[:], misc[:], xh[:], ALU.subtract).then_inc(xl_done, 1)
                    if j == 1 and has(it, 3):
                        dve.wait_ge(x_loaded, 16 * upto(it, 3))
                        for tt in range(KT):
                            nc.vector.bn_stats(stats[:, tt, :], xt[:, b, tt, :]).then_inc(stats_done, 1)
                        dve.wait_ge(stats_done, held(dve, KT * upto(it, 3)))
                        for tt in range(KT):
                            nc.vector.bn_aggr(mv[:, tt, :], stats[:, tt, :]).then_inc(mv_done, 1)
                    if j == 1 and has(it, -2):
                        dve.wait_ge(rstd2_done, upto(it, -2))
                        dve.wait_ge(ln_stored, 16 * upto(it, -3))
                        for tt in range(KT):
                            nc.vector.tensor_scalar(ln[:, tt, :], y[:, tt, :], mv2[:, tt, 0:1], rstd2[:, tt:tt + 1],
                                                    ALU.subtract, ALU.mult).then_inc(ln_done, 1)
                        dve.wait_ge(ln_done, KT * upto(it, -2))
                        nc.vector.tensor_reduce(t["lnmax"][:], ln[:], AX.XY, ALU.max,
                                                apply_absolute_value=True).then_inc(lmax_tmp, 1)
                        dve.wait_ge(lmax_tmp, upto(it, -2))
                        dve.wait_ge(lmax_done, upto(it, -2))
                        nc.vector.tensor_tensor(lmax[:], lmax[:], t["lnmax"][:], ALU.max).then_inc(lmax_done, 1)
                    if j == 2 and has(it, -1):
                        dve.wait_ge(den_loaded, 16 * upto(it, -1))
                        dve.wait_ge(rec_written, 16 * upto(it, -2))
                        nc.vector.reciprocal(rec[:], den[:]).then_inc(rec_done, 1)
                    if j == 2 and has(it, 2):
                        dve.wait_ge(ch_done, upto(it, 2))
                        nc.vector.tensor_tensor(cl[:], misc[:], ch[:], ALU.subtract).then_inc(cl_done, 1)
                    if j == 3 and has(it, 2):
                        dve.wait_ge(qh_done, upto(it, 2))
                        low(0, ql_done)
                    if j == 4 and has(it, 2):
                        dve.wait_ge(kh_done, upto(it, 2))
                        low(1, kl_done)
                    if j == 4 and has(it, 3):
                        dve.wait_ge(rstd_done, upto(it, 3))
                        dve.wait_ge(xt_done, upto(it, 2))
                        for tt in range(KT):
                            op = nc.vector.tensor_scalar(xn[:, tt, :], xt[:, b, tt, :], mv[:, tt, 0:1],
                                                         rstd[:, tt:tt + 1], ALU.subtract, ALU.mult)
                        op.then_inc(xn_ready, 1)
                    if j == 6 and has(it, 2):
                        dve.wait_ge(v_done, upto(it, 2))
                        dve.wait_ge(pv_done, 4 * upto(it, -1))
                        for tt in range(KT):
                            op = nc.vector.scalar_tensor_tensor(
                                out=vt[:, (b + 2) % 3, tt, :, 0:HD], in0=misc[:, tt, :].rearrange("p (h j) -> p h j", j=HD),
                                scalar=1.0 / WS, in1=bv[:].rearrange("p (h j) -> p h j", j=HD), op0=ALU.mult, op1=ALU.add)
                        op.then_inc(v_taken, 1)
                    if j == 7 and has(it, -1):
                        dve.wait_ge(o_done, upto(it, -1))
                        dve.wait_ge(xb_done, upto(it, -1))
                        dve.wait_ge(y_stored, 16 * upto(it, -2))
                        dve.wait_ge(ln_done, KT * upto(it, -2))
                        nc.vector.scalar_tensor_tensor(out=y[:], in0=misc[:], scalar=tgs[:, 0:1], in1=xb[:],
                                                       op0=ALU.mult, op1=ALU.add).then_inc(y_done, 1)
                        dve.wait_ge(y_done, upto(it, -1))
                        for tt in range(KT):
                            nc.vector.bn_stats(stats2[:, tt, :], y[:, tt, :]).then_inc(stats2_done, 1)
                        dve.wait_ge(stats2_done, held(dve, KT * upto(it, -1)))
                        for tt in range(KT):
                            nc.vector.bn_aggr(mv2[:, tt, :], stats2[:, tt, :]).then_inc(mv2_done, 1)
                    if has(it, 1):
                        for tt in range(KT):
                            dve.wait_ge(s_done, count(16 * (it + 1) + 2 * j + tt + 1))
                            lo = 8 * (j // 4) + j % 4
                            nc.vector.tensor_reduce(negm[:, (b + 1) % 3, tt, lo:lo + 5:4], s_ps[tt][:], AX.X, ALU.max,
                                                    negate=True).then_inc(max_done, 1)

            iterations(nc.vector, body)

        @block.gpsimd
        def _(pool):
            nc.gpsimd.memset(ident[:], 0.0).then_inc(ident_set, 1)
            pool.wait_ge(ident_set, 1)
            nc.gpsimd.affine_select(out=ident[:], in_=ident[:], compare_op=ALU.not_equal, fill=1.0, base=0,
                                    pattern=[[-1, P]], channel_multiplier=1).then_inc(ident_set, 1)
            nc.gpsimd.memset(vt[:, :, :, :, HD:32], 0.0).then_inc(ident_set, 1)
            pool.wait_ge(ident_set, 3)
            nc.gpsimd.memset(vt[:, :, :, :, HD:HD + 1], 1.0).then_inc(consts_set, 1)
            pool.wait_ge(consts_set, 4)
            pool.wait_ge(gate_scaled, 2)

            def root(var, eps_out, out_, first, second, batches):
                nc.gpsimd.tensor_scalar(eps_out[:], var, EPS, 1.0, ALU.add, ALU.mult).then_inc(first, 1)
                pool.wait_ge(first, held(pool, batches))
                nc.gpsimd.tensor_tensor(out_[:], eps_out[:], half[:], ALU.pow).then_inc(second, 1)

            def body(it, b):
                n = (b + 2) % 3
                if has(it, -2):
                    pool.wait_ge(mv2_done, held(pool, KT * upto(it, -2)))
                    root(mv2[:, :, 1], ve2, rstd2, ve2_done, rstd2_done, upto(it, -2))
                if has(it, 3):
                    pool.wait_ge(mv_done, held(pool, KT * upto(it, 3)))
                    root(mv[:, :, 1], ve, rstd, ve_done, rstd_done, upto(it, 3))
                if has(it, -1):
                    pool.wait_ge(xr_loaded, held(pool, 16 * upto(it, -1)))
                    pool.wait_ge(y_done, held(pool, upto(it, -2)))
                    nc.gpsimd.tensor_tensor(xb[:], xr[:], tbo[:].rearrange("p (o d) -> p o d", o=1).broadcast_to((P, KT, D)),
                                            ALU.add).then_inc(xb_done, 1)
                    pool.wait_ge(rec_loaded, held(pool, 16 * upto(it, -1)))
                    pool.wait_ge(al_done, held(pool, upto(it, -2)))
                    nc.gpsimd.tensor_tensor(at[:], ot[:, n], recb[:], ALU.mult).then_inc(at_done, 1)
                    pool.wait_ge(ah_done, held(pool, upto(it, -1)))
                    pool.wait_ge(o_done, held(pool, upto(it, -2)))
                    nc.gpsimd.tensor_tensor(al[:], at[:], ah[:], ALU.subtract).then_inc(al_done, 1)

            iterations(nc.gpsimd, body)
            pool.wait_ge(lmax_done, NB + 1)
            nc.gpsimd.partition_all_reduce(t["lmaxall"][:], lmax[:], P, RMAX).then_inc(lmax_tmp, 1)
            pool.wait_ge(lmax_tmp, NB + 1)


def feed_forward(nc, t, out):
    NB, S, D = out.shape
    F = t["w_gate"].shape[0]
    KT = S // P
    DT = D // P
    FT = F // P
    CB = 2
    CW = CB * S
    NC = NB // CB
    PR = FT // 2
    NBLK = D // 32
    ov = out.rearrange("b (p t) d -> b p t d", t=KT)

    with ExitStack() as es:
        def sb(name, shape, dt):
            return es.enter_context(nc.sbuf_tensor(name, shape, dt))

        def sem(name):
            return es.enter_context(nc.semaphore(name))

        ident = sb("ident16", [P, P], F16)
        wgt = sb("wgt", [P, 2, DT, F], F16)
        wut = sb("wut", [P, 2, DT, F], F16)
        wdt = sb("wdt", [P, 2, FT, D], F16)
        xq = sb("xq", [P, 2, NC, DT, CW], F16)
        scal = sb("scal", [P, 32], F32)
        gx = sb("gf", [P, 1], F32)
        cmax = sb("cmax", [P, 4, NC * PR], F32)
        vmax = sb("vmax", [P, 4, 2], F32)
        ps = es.enter_context(nc.psum_tensor("pairs", [P, 4, 2, CW], F32))

        id_set = sem("f_id_set")
        wn_loaded = sem("f_wn_loaded")
        blk_max = sem("f_blk_max")
        blk_scaled = sem("f_blk_scaled")
        blk_inv = sem("f_blk_inv")
        w_int = sem("f_w_int")
        w_clipped = sem("f_w_clipped")
        w_real = sem("f_w_real")
        w_high = sem("f_w_high")
        w_low = sem("f_w_low")
        w_turned = sem("f_w_turned")
        w_kept = sem("f_w_kept")
        gf_loaded = sem("f_gf_loaded")
        gf_tanh = sem("f_gf_tanh")
        x_int = sem("f_x_int")
        xt_turned = sem("f_xt_turned")
        xt_high = sem("f_xt_high")
        xt_low = sem("f_xt_low")
        chain = sem("f_chain")
        all_max = sem("f_all_max")
        g_done = sem("f_g_done")
        g_kept = sem("f_g_kept")
        g_max = sem("f_g_max")
        qg_done = sem("f_qg_done")
        sig_done = sem("f_sig_done")
        sq_done = sem("f_sq_done")
        p2_done = sem("f_p2_done")
        p2_max = sem("f_p2_max")
        u_done = sem("f_u_done")
        u_max = sem("f_u_max")
        u2_done = sem("f_u2_done")
        qu_done = sem("f_qu_done")
        q2_done = sem("f_q2_done")
        p3_done = sem("f_p3_done")
        p3_max = sem("f_p3_max")
        q3_done = sem("f_q3_done")
        h3_done = sem("f_h3_done")
        l3_done = sem("f_l3_done")
        d_done = sem("f_d_done")
        z_done = sem("f_z_done")
        y_loaded = [sem(f"f_y_loaded{d}") for d in range(2)]
        z_stored = [sem(f"f_z_stored{d}") for d in range(2)]
        counts = {e.engine: e.alloc_register("count_ffn") for e in (nc.gpsimd, nc.sync, nc.scalar, nc.vector)}

        def held(eng, n):
            if isinstance(n, int):
                return n
            eng.reg_mov(counts[eng.engine], n)
            eng.wait_ge(id_set, 1)
            return counts[eng.engine]

        SX, KX, SG, KG, SU, KU, S2, K2, S3, K3, TG, KD, TMP = range(13)

        def col(k):
            return scal[:, k:k + 1]

        with ExitStack() as ws:
            def wb(name, shape, dt):
                return ws.enter_context(nc.sbuf_tensor(name, shape, dt))
            NW = FT * D
            wn = wb("wn", [P, 3, NW], F32)
            wi = wb("wi", [P, 3, NW], I16)
            bm = wb("bm", [P, 3, NW // 32], F32)
            bs = wb("bs", [P, 3, NW // 32], F32)
            bi = wb("bi", [P, 3, NW // 32], F32)
            wq2 = wb("wq2", [P, 2, 3, NW], F16)
            xi = wb("xi", [P, NB, KT, D], I16)
            block = ws.enter_context(nc.Block())

            @block.sync
            def _(sp):
                for i, n in enumerate(("w_gate", "w_up")):
                    sp.dma_start(wn[:, i].rearrange("p (f d) -> p f d", d=D),
                                 t[n].rearrange("(f p) d -> p f d", p=P)).then_inc(wn_loaded, 16)
                sp.dma_start(wn[:, 2].rearrange("p (o f) -> p o f", f=F),
                             t["w_down"].rearrange("(o p) f -> p o f", p=P)).then_inc(wn_loaded, 16)
                sp.dma_start(gx[:], t["gf"].rearrange("(o d) -> o d", o=1).broadcast_to((P, 1))).then_inc(gf_loaded, 16)

            @block.gpsimd
            def _(pool):
                nc.gpsimd.memset(ident[:], 0.0).then_inc(id_set, 1)
                pool.wait_ge(id_set, 1)
                nc.gpsimd.affine_select(out=ident[:], in_=ident[:], compare_op=ALU.not_equal, fill=1.0, base=0,
                                        pattern=[[-1, P]], channel_multiplier=1).then_inc(id_set, 1)

            @block.vector
            def _(dve):
                nc.vector.tensor_scalar(col(SX), t["lmaxall"][:], 1.0 / QMAX, 1e-12, ALU.mult, ALU.max).then_inc(chain, 1)
                dve.wait_ge(chain, 1)
                nc.vector.reciprocal(col(KX), col(SX)).then_inc(chain, 1)
                dve.wait_ge(chain, 2)
                for h in range(4):
                    nb = NB // 4
                    nc.vector.tensor_scalar(xi[:, h * nb:(h + 1) * nb].rearrange("p b t d -> p (b t d)"),
                                            t["lnall"][:, h * nb:(h + 1) * nb].rearrange("p b c -> p (b c)"),
                                            col(KX), None, ALU.mult).then_inc(x_int, 1)
                dve.wait_ge(wn_loaded, 48)
                w3 = wn[:].rearrange("p i (k w) -> p (i k) w", w=32)
                nc.vector.tensor_reduce(bm[:].rearrange("p i k -> p (i k)"), w3, AX.X, ALU.max,
                                        apply_absolute_value=True).then_inc(blk_max, 1)
                dve.wait_ge(blk_max, 1)
                nc.vector.tensor_scalar(bs[:], bm[:], 1.0 / 7.0, 1e-12, ALU.mult, ALU.max).then_inc(blk_scaled, 1)
                dve.wait_ge(blk_scaled, 1)
                nc.vector.reciprocal(bi[:], bs[:]).then_inc(blk_inv, 1)
                dve.wait_ge(blk_inv, 1)
                nc.vector.tensor_scalar(bs[:], bs[:], FS, None, ALU.mult).then_inc(blk_scaled, 1)

                def wide(a, i):
                    return a[:, i].rearrange("p (k o) -> p k o", o=1).broadcast_to((P, NW // 32, 32))

                def blocks(a):
                    return a.rearrange("p (k w) -> p k w", w=32)

                for i in range(3):
                    nc.vector.tensor_tensor(blocks(wi[:, i]), blocks(wn[:, i]), wide(bi, i), ALU.mult).then_inc(w_int, 1)
                dve.wait_ge(w_int, 3)
                for i in range(3):
                    nc.vector.tensor_scalar(wi[:, i], wi[:, i], 7.0, -8.0, ALU.min, ALU.max).then_inc(w_clipped, 1)
                dve.wait_ge(w_clipped, 3)
                dve.wait_ge(blk_scaled, 2)
                for i in range(3):
                    nc.vector.tensor_tensor(blocks(wn[:, i]), blocks(wi[:, i]), wide(bs, i), ALU.mult).then_inc(w_real, 1)
                for i in range(3):
                    dve.wait_ge(w_high, i + 1)
                    nc.vector.tensor_tensor(wq2[:, 1, i], wn[:, i], wq2[:, 0, i], ALU.subtract).then_inc(w_low, 1)
                for c in range(NC):
                    dve.wait_ge(xt_high, c + 1)
                    nc.vector.tensor_tensor(xq[:, 1, c], ps[:, c % 2, 0].bitcast(I16).rearrange("p (d w) -> p d w", d=DT),
                                            xq[:, 0, c], ALU.subtract).then_inc(xt_low, 1)

            @block.scalar
            def _(act):
                act.wait_ge(gf_loaded, 16)
                nc.scalar.activation(col(TG), gx[:], ACT.Tanh).then_inc(gf_tanh, 1)
                for i in range(3):
                    act.wait_ge(w_real, i + 1)
                    nc.scalar.copy(wq2[:, 0, i], wn[:, i]).then_inc(w_high, 1)
                for c in range(NC):
                    act.wait_ge(xt_turned, c + 1)
                    nc.scalar.copy(xq[:, 0, c], ps[:, c % 2, 0].bitcast(I16).rearrange("p (d w) -> p d w", d=DT)
                                   ).then_inc(xt_high, 1)
                for k in range(12):
                    act.wait_ge(w_turned, k + 1)
                    i, r = k // 4, k % 4
                    bank = ps[:, 2 + k % 2, 0].bitcast(F16)[:, 0:F]
                    if i < 2:
                        dst = (wgt, wut)[i][:, r // 2, r % 2]
                    else:
                        dst = wdt[:, r // 2, 3 * (r % 2):3 * (r % 2) + 3].rearrange("p f d -> p (f d)")
                    nc.scalar.copy(dst, bank).then_inc(w_kept, 1)

            @block.tensor
            def _(pe):
                pe.wait_ge(id_set, 2)
                for c in range(NC):
                    pe.wait_ge(x_int, c * CB // (NB // 4) + 1)
                    pe.wait_ge(xt_low, max(c - 1, 0))
                    bank = ps[:, c % 2, 0].bitcast(F16)
                    for d in range(DT):
                        for k in range(CB * KT):
                            mm = nc.tensor.transpose(bank[:, d * CW + k * P:d * CW + (k + 1) * P],
                                                     xi[:, c * CB + k // KT, k % KT, d * P:(d + 1) * P].bitcast(F16), ident[:])
                    mm.then_inc(xt_turned, 1)
                for k in range(12):
                    i, r = k // 4, k % 4
                    pe.wait_ge(w_high, 3)
                    pe.wait_ge(w_low, 3)
                    pe.wait_ge(w_kept, max(k - 1, 0))
                    bank = ps[:, 2 + k % 2, 0].bitcast(F16)
                    part = r // 2
                    for f in range(6):
                        if i < 2:
                            src = wq2[:, part, i, f * D + (r % 2) * P:f * D + (r % 2 + 1) * P]
                        else:
                            ft, o = 3 * (r % 2) + f // 2, f % 2
                            src = wq2[:, part, 2, o * F + ft * P:o * F + (ft + 1) * P]
                        mm = nc.tensor.transpose(bank[:, f * P:(f + 1) * P], src, ident[:])
                    mm.then_inc(w_turned, 1)

        with ExitStack() as ws:
            def wb(name, shape, dt):
                return ws.enter_context(nc.sbuf_tensor(name, shape, dt))
            gb = wb("gb", [P, NC, FT, CW], F32)
            h3 = wb("h3", [P, 2, FT, CW], F16)
            words = t["lnall"]
            ia = words[:, 0:6, :].rearrange("p b c -> p (b c)").bitcast(I16).rearrange("p (d f w) -> p d f w", d=2, f=FT)
            ib = words[:, 6:12, :].rearrange("p b c -> p (b c)").bitcast(I16).rearrange("p (d f w) -> p d f w", d=2, f=FT)
            yb = words[:, 12:16, :].rearrange("p (d b) c -> p d b c", d=2)
            block = ws.enter_context(nc.Block())

            def rounds(eng, body):
                with eng.Fori(0, NC - 1, 2) as i:
                    for d in range(2):
                        body(i + d, d)

            @block.tensor
            def _(pe):
                def project(w, done, free):
                    def body(c, d):
                        for p in range(PR):
                            pe.wait_ge(free, PR * c + p + 1)
                            for k in range(2):
                                f = 2 * p + k
                                terms = [(a, b, dt) for a, b in ((0, 0), (0, 1), (1, 0)) for dt in range(DT)]
                                for n, (a, b, dt) in enumerate(terms):
                                    mm = nc.tensor.matmul(ps[:, p, k, :], w[:, a, dt, f * P:(f + 1) * P],
                                                          xq[:, b, c, dt, :], start=n == 0, stop=n == len(terms) - 1)
                            mm.then_inc(done, 1)
                    rounds(nc.tensor, body)

                project(wgt, g_done, g_kept)
                pe.wait_ge(g_kept, PR * NC + PR)
                project(wut, u_done, u_max)
                pe.wait_ge(u_max, PR * NC + PR)
                project(wut, u2_done, qu_done)
                pe.wait_ge(qu_done, PR * NC + PR)

                def down(c, d):
                    pe.wait_ge(h3_done, c + 1)
                    pe.wait_ge(l3_done, c + 1 + 2)
                    for b in range(CB):
                        pe.wait_ge(z_done, CB * c + b + 1)
                        for tt in range(KT):
                            tok = (b * KT + tt) * P
                            terms = [(l, h, f) for l, h in ((0, 0), (0, 1), (1, 0)) for f in range(FT)]
                            for n, (l, h, f) in enumerate(terms):
                                src = (h3, ia)[l]
                                lh = src[:, d, f, tok:tok + P]
                                if l:
                                    lh = lh.bitcast(F16)
                                mm = nc.tensor.matmul(ps[:, 3, b, tt * D:(tt + 1) * D], lh, wdt[:, h, f, :],
                                                      start=n == 0, stop=n == len(terms) - 1)
                        mm.then_inc(d_done, 1)
                pe.sem_inc(d_done, 2 * CB)
                rounds(nc.tensor, down)

            @block.scalar
            def _(act):
                def keep(c, d):
                    for p in range(PR):
                        act.wait_ge(g_done, held(act, PR * c + p + 1))
                        nc.scalar.copy(gb[:, c, 2 * p:2 * p + 2, :], ps[:, p]).then_inc(g_kept, 1)
                act.sem_inc(g_kept, PR)
                act.sem_inc(qu_done, PR)
                rounds(nc.scalar, keep)
                act.wait_ge(chain, 2 + 4)

                def gate(c, d):
                    act.wait_ge(p2_done, c - 1 + 2)
                    nc.scalar.activation(ia[:, d], gb[:, c], ACT.Copy, scale=col(KG)).then_inc(qg_done, 1)
                    act.wait_ge(qg_done, held(act, c + 1))
                    nc.scalar.activation(gb[:, c], ia[:, d], ACT.Sigmoid, scale=col(SG)).then_inc(sig_done, 1)
                    act.wait_ge(sig_done, held(act, c + 1))
                    nc.scalar.activation(ib[:, d].bitcast(U16), gb[:, c], ACT.Copy, scale=LEVELS).then_inc(sq_done, 1)
                rounds(nc.scalar, gate)
                act.wait_ge(chain, 2 + 4 + 4 + 4)

                def products(c, d):
                    act.wait_ge(p3_done, c - 1 + 2)
                    for p in range(PR):
                        act.wait_ge(u2_done, PR * c + p + 1)
                        nc.scalar.activation(ia[:, d, 2 * p:2 * p + 2, :], ps[:, p], ACT.Copy, scale=col(KU)
                                             ).then_inc(qu_done, 1)
                    nc.scalar.activation(ib[:, d], gb[:, c], ACT.Copy, scale=col(K2)).then_inc(q2_done, 1)
                rounds(nc.scalar, products)
                act.wait_ge(chain, 2 + 4 + 4 + 4 + 4)

                def last(c, d):
                    act.wait_ge(l3_done, c - 1 + 2)
                    nc.scalar.activation(ib[:, d], gb[:, c], ACT.Copy, scale=col(K3)).then_inc(q3_done, 1)
                rounds(nc.scalar, last)

            @block.vector
            def _(dve):
                links = [2]

                def linked(op):
                    op.then_inc(chain, 1)
                    links[0] += 1
                    dve.wait_ge(chain, links[0])

                def scale(m, unit, imm, s, k):
                    linked(nc.vector.tensor_scalar(col(TMP), m, unit, imm / QMAX, ALU.mult, ALU.mult))
                    linked(nc.vector.tensor_scalar(col(s), col(TMP), 1e-12, None, ALU.max))
                    linked(nc.vector.reciprocal(col(TMP), col(s)))
                    linked(nc.vector.tensor_scalar(col(k), col(TMP), unit, imm, ALU.mult, ALU.mult))

                dve.sem_inc(u_max, PR)
                dve.sem_inc(p2_done, 2)
                dve.sem_inc(p3_done, 2)
                dve.sem_inc(l3_done, 2)
                dve.sem_inc(z_done, CB)

                def whole(i, width):
                    nc.vector.tensor_reduce(vmax[:, i, 0:1], cmax[:, i, 0:width], AX.X, ALU.max).then_inc(g_max, 1)

                def gmax(c, d):
                    dve.wait_ge(g_kept, PR * c + PR + PR)
                    nc.vector.tensor_reduce(cmax[:, 0, bass.ds(c, 1)], gb[:, c], AX.XY, ALU.max,
                                            apply_absolute_value=True).then_inc(g_max, 1)
                rounds(nc.vector, gmax)
                dve.wait_ge(g_max, NC)
                whole(0, NC)
                dve.wait_ge(all_max, 1)
                scale(vmax[:, 0, 1:2], col(SX), 1.0 / FS, SG, KG)

                def gate(c, d):
                    for p in range(PR):
                        dve.wait_ge(u_done, PR * c + p + 1)
                        nc.vector.tensor_reduce(cmax[:, 1, bass.ds(PR * c + p, 1)], ps[:, p], AX.XY, ALU.max,
                                                apply_absolute_value=True).then_inc(u_max, 1)
                    dve.wait_ge(sq_done, c + 1)
                    nc.vector.tensor_tensor(gb[:, c], ia[:, d], ib[:, d].bitcast(U16), ALU.mult).then_inc(p2_done, 1)
                    dve.wait_ge(p2_done, c + 1 + 2)
                    nc.vector.tensor_reduce(cmax[:, 2, bass.ds(c, 1)], gb[:, c], AX.XY, ALU.max,
                                            apply_absolute_value=True).then_inc(p2_max, 1)
                rounds(nc.vector, gate)
                dve.wait_ge(u_max, PR * NC + PR)
                whole(1, PR * NC)
                dve.wait_ge(p2_max, NC)
                whole(2, NC)
                dve.wait_ge(all_max, 2)
                scale(vmax[:, 1, 1:2], col(SX), 1.0 / FS, SU, KU)
                dve.wait_ge(all_max, 3)
                scale(vmax[:, 2, 1:2], col(SG), 1.0 / LEVELS, S2, K2)

                def products(c, d):
                    dve.wait_ge(qu_done, PR * c + PR + PR)
                    dve.wait_ge(q2_done, c + 1)
                    nc.vector.tensor_tensor(gb[:, c], ia[:, d], ib[:, d], ALU.mult).then_inc(p3_done, 1)
                    dve.wait_ge(p3_done, c + 1 + 2)
                    nc.vector.tensor_reduce(cmax[:, 3, bass.ds(c, 1)], gb[:, c], AX.XY, ALU.max,
                                            apply_absolute_value=True).then_inc(p3_max, 1)
                rounds(nc.vector, products)
                dve.wait_ge(p3_max, NC)
                whole(3, NC)
                dve.wait_ge(all_max, 4)
                nc.vector.tensor_tensor(col(KD), col(S2), col(SU), ALU.mult).then_inc(p3_max, 1)
                dve.wait_ge(p3_max, NC + 1)
                scale(vmax[:, 3, 1:2], col(KD), 1.0, S3, K3)
                dve.wait_ge(gf_tanh, 1)
                linked(nc.vector.tensor_scalar(col(KD), col(S3), col(TG), 1.0 / FS, ALU.mult, ALU.mult))

                def last(c, d):
                    dve.wait_ge(q3_done, c + 1)
                    dve.wait_ge(d_done, CB * c + CB)
                    nc.vector.tensor_copy(h3[:, d], ib[:, d]).then_inc(h3_done, 1)
                    dve.wait_ge(h3_done, c + 1)
                    nc.vector.tensor_tensor(ia[:, d].bitcast(F16), ib[:, d], h3[:, d], ALU.subtract).then_inc(l3_done, 1)
                    for b in range(CB):
                        dve.wait_ge(y_loaded[d], 8 * (c - d) + 16)
                        dve.wait_ge(d_done, CB * c + b + 1 + 2 * CB)
                        nc.vector.scalar_tensor_tensor(out=yb[:, d, b, :], in0=ps[:, 3, b, :], scalar=col(KD),
                                                       in1=yb[:, d, b, :], op0=ALU.mult, op1=ALU.add).then_inc(z_done, 1)
                rounds(nc.vector, last)

            @block.gpsimd
            def _(pool):
                for i in range(4):
                    pool.wait_ge(g_max, held(pool, NC + 1 + i))
                    nc.gpsimd.partition_all_reduce(vmax[:, i, 1:2], vmax[:, i, 0:1], P, RMAX).then_inc(all_max, 1)

                def body(c, d):
                    pool.wait_ge(z_stored[d], held(pool, 8 * CB * (c - d) + 16))
                    pool.dma_start(yb[:, d], ov[bass.ds(CB * c, CB)].rearrange("b p t d -> p b (t d)")
                                   ).then_inc(y_loaded[d], 16)
                rounds(nc.gpsimd, body)

            @block.sync
            def _(sp):
                def body(c, d):
                    for b in range(CB):
                        sp.wait_ge(z_done, held(sp, CB * c + b + 1 + CB))
                        sp.dma_start(ov[CB * c + b], yb[:, d, b].rearrange("p (t d) -> p t d", t=KT)
                                     ).then_inc(z_stored[d], 16)
                for d in range(2):
                    sp.sem_inc(z_stored[d], 16)
                rounds(nc.sync, body)
                for d in range(2):
                    sp.wait_ge(z_stored[d], held(sp, 16 * NB // 2 + 16))



def build(nc, a, out):
    NB, S, D = out.shape
    with ExitStack() as es:
        a["lnall"] = es.enter_context(nc.sbuf_tensor("lnall", [P, NB, S // P * D], F32))
        a["lnmax"] = es.enter_context(nc.sbuf_tensor("lnmax", [P, 1], F32))
        a["lmaxall"] = es.enter_context(nc.sbuf_tensor("lmaxall", [P, 1], F32))
        attention(nc, a, a["x"], a["ctx"], out)
        feed_forward(nc, a, out)


def kernel(x, ctx_1024, g_xattn, g_ffn, L0_xattn_Wq, L0_xattn_bq, L0_xattn_Wk, L0_xattn_bk, L0_xattn_Wv, L0_xattn_bv,
           L0_xattn_Wo, L0_xattn_bo, L0_ffn_w_gate, L0_ffn_w_up, L0_ffn_w_down):
    import numpy as np
    import concourse.bacc as bacc
    from concourse.bass_utils import run_bass_kernel_spmd

    def columns(v):
        return np.asarray(v).reshape(-1, P).T

    arrays = {
        "x": x, "ctx": ctx_1024, "gx": g_xattn, "gf": g_ffn,
        "wq": np.asarray(L0_xattn_Wq).T, "wk": np.asarray(L0_xattn_Wk).T, "wv": np.asarray(L0_xattn_Wv).T,
        "wo": np.asarray(L0_xattn_Wo).T, "bq": columns(L0_xattn_bq), "bk": columns(L0_xattn_bk),
        "bv": L0_xattn_bv, "bo": L0_xattn_bo,
        "w_gate": L0_ffn_w_gate, "w_up": L0_ffn_w_up, "w_down": L0_ffn_w_down,
    }
    nc = bacc.Bacc("TRN2", target_bir_lowering=False, num_devices=1)
    feed, aps = {}, {}
    for name, a in arrays.items():
        a = np.ascontiguousarray(a)
        feed["in_" + name] = a
        aps[name] = nc.dram_tensor("in_" + name, a.shape, mybir.dt.from_np(a.dtype), kind="ExternalInput").ap()
    out = nc.dram_tensor("out_0", x.shape, F32, kind="ExternalOutput").ap()
    build(nc, aps, out)
    r = run_bass_kernel_spmd(nc, [feed], core_ids=[0])
    return r.results[0]["out_0"]
```

```python
from contextlib import ExitStack

import concourse.bass as bass
from concourse import mybir

ALU = mybir.AluOpType
ACT = mybir.ActivationFunctionType
AX = mybir.AxisListType
F32 = mybir.dt.float32
F16 = mybir.dt.float16
I16 = mybir.dt.int16
U16 = mybir.dt.uint16
RMAX = bass.bass_isa.ReduceOp.absmax

P = 128
EPS = 1e-5
WS = 16.0
FS = 256.0
MS = 64.0
HD = 16
NH = 16
PAIRS = NH // 2
QMAX = 32767.0
BLOCK = 32
LEVELS = 65536.0


def attention(nc, t, x, ctx, out):
    NB, S, D = x.shape
    KT = S // P
    UNITS = PAIRS * KT
    SPAN = range(-3, NB + 2)
    FIRST = 3
    LAST = FIRST + 3 * ((NB - 4 - FIRST) // 3) - 1

    xv = x.rearrange("b (p t) d -> b p t d", t=KT)
    cv = ctx.rearrange("b (p t) d -> b p t d", t=KT)
    ov = out.rearrange("b (p t) d -> b p t d", t=KT)

    qk_dram = nc.dram_tensor("qk_dram", (3, 4, 2, HD, 4 * KT * S), F16, kind="Internal").ap()
    rec_dram = nc.dram_tensor("rec_dram", (3, 4, 4 * S), F32, kind="Internal").ap()

    with ExitStack() as es:
        def sb(name, shape, dt):
            return es.enter_context(nc.sbuf_tensor(name, shape, dt))

        def pb(name, shape, dt):
            return es.enter_context(nc.psum_tensor(name, shape, dt))

        def sem(name):
            return es.enter_context(nc.semaphore(name))

        ident = sb("ident", [P, P], F32)
        wfall = sb("wfall", [P, 3, 2, D], F32)
        wf = {n: wfall[:, i] for i, n in enumerate("qkv")}
        wh = {n: sb("wh_" + n, [P, 2, D], F16) for n in "qkv"}
        wl = {n: sb("wl_" + n, [P, 2, D], F16) for n in "qkv"}
        wof = sb("wof", [P, 4, D], F32)
        woh = sb("woh", [P, 4, D], F16)
        wol = sb("wol", [P, 4, D], F16)
        bqk = sb("bqk", [P, 2, 2], F32)
        bqk_s = sb("bqk_s", [P, 2, 2], F32)
        bvc = sb("bvc", [P, 4], F32)
        bo = sb("bo", [P, D], F32)
        tbo = sb("tbo", [P, D], F32)
        gx = sb("gx", [P, 1], F32)
        gf = sb("gf", [P, 1], F32)
        tg = sb("tg", [P, 1], F32)
        tgs = sb("tgs", [P, 1], F32)
        half = sb("half", [P, KT], F32)

        xt = sb("xt", [P, 3, KT, D], F32)
        ct = sb("ct", [P, KT, D], F32)
        xn = sb("xn", [P, KT, D], F32)
        stats = sb("stats", [P, KT, 6], F32)
        mv = sb("mv", [P, KT, 2], F32)
        ve = sb("ve", [P, KT], F32)
        rstd = sb("rstd", [P, KT], F32)
        xh = sb("xh", [P, 2, S], F16)
        xl = sb("xl", [P, 2, S], F16)
        ch = sb("ch", [P, 2, S], F16)
        cl = sb("cl", [P, 2, S], F16)
        qk = sb("qk", [P, 4, 2, S], F16)
        kst = sb("kst", [97, 3, PAIRS, S], F16)
        qst = sb("qst", [97, 3, 2, PAIRS, S], F16)
        vt = sb("vt", [P, 3, KT, NH, 32], F32)
        negm = sb("negm", [P, 3, KT, NH], F32)
        mrow = sb("mrow", [8, 2, S], F16)
        pt = sb("pt", [P, 2, 2, KT, 2, S], F32)
        ot = sb("ot", [P, 3, 4, S], F32)
        den = sb("den", [P, 32], F32)
        rec = sb("rec", [P, 32], F32)
        recb = sb("recb", [P, 4, S], F32)
        at = sb("at", [P, 4, S], F32)
        bvw = at[:, :, 0:P]
        ah = sb("ah", [P, 4, S], F16)
        al = sb("al", [P, 4, S], F16)
        xr = sb("xr", [P, KT, D], F32)
        xb = sb("xb", [P, KT, D], F32)
        y = sb("y", [P, KT, D], F32)
        stats2 = sb("stats2", [P, KT, 6], F32)
        mv2 = sb("mv2", [P, KT, 2], F32)
        ve2 = sb("ve2", [P, KT], F32)
        rstd2 = sb("rstd2", [P, KT], F32)
        ln = sb("ln", [P, KT, D], F32)
        lmax = sb("lmax", [P, 1], F32)

        F = t["w_gate"].shape[0]
        NW = F * D // P
        NBLK = NW // BLOCK
        wn = [wfall[:].rearrange("p n t d -> p (n t d)"), xt[:].rearrange("p b t d -> p (b t d)")]
        wn.append(wn[0])
        wi = sb("wi", [P, NW], I16)
        bm = sb("bm", [P, NBLK], F32)
        bs = sb("bs", [P, NBLK], F32)
        bi = sb("bi", [P, NBLK], F32)
        bf = sb("bf", [P, NBLK], F32)
        wq = sb("wq", [P, 2, 2, NW], F16)

        s_ps = [pb(f"s_ps{i}", [P, 2, S], F32) for i in range(2)]
        st_ps = [pb(f"st_ps{i}", [P, 2, S], F32) for i in range(3)]
        pv_ps = pb("pv_ps", [P, 2, S], F32)
        misc = [pb(f"misc{i}", [P, 2, S], F32) for i in range(2)]

        ident_set = sem("ident_set")
        consts_set = sem("consts_set")
        w_loaded = sem("w_loaded")
        wo_loaded = sem("wo_loaded")
        bv_spread = sem("bv_spread")
        ident16_set = sem("ident16_set")
        wn_loaded = sem("wn_loaded")
        blk_max = sem("blk_max")
        blk_scaled = sem("blk_scaled")
        blk_inv = sem("blk_inv")
        w_int = sem("w_int")
        w_clipped = sem("w_clipped")
        w_real = sem("w_real")
        w_high = sem("w_high")
        w_low = sem("w_low")
        w_turned = sem("w_turned")
        w_kept = sem("w_kept")
        bvo_done = sem("bvo_done")
        b_loaded = sem("b_loaded")
        g_loaded = sem("g_loaded")
        wo_zeroed = sem("wo_zeroed")
        weights_split = sem("weights_split")
        gate_done = sem("gate_done")
        gate_scaled = sem("gate_scaled")
        bias_ready = sem("bias_ready")
        x_loaded = sem("x_loaded")
        c_loaded = sem("c_loaded")
        stats_done = sem("stats_done")
        mv_done = sem("mv_done")
        ve_done = sem("ve_done")
        rstd_done = sem("rstd_done")
        xn_ready = sem("xn_ready")
        xt_done = sem("xt_done")
        xh_done = sem("xh_done")
        xl_done = sem("xl_done")
        ct_done = sem("ct_done")
        ch_done = sem("ch_done")
        cl_done = sem("cl_done")
        q_done = sem("q_done")
        qh_done = sem("qh_done")
        ql_done = sem("ql_done")
        k_done = sem("k_done")
        kh_done = sem("kh_done")
        kl_done = sem("kl_done")
        q_written = sem("q_written")
        k_written = sem("k_written")
        stack_loaded = sem("stack_loaded")
        s_done = sem("s_done")
        max_done = sem("max_done")
        mt_done = sem("mt_done")
        mh_done = sem("mh_done")
        ma_loaded = sem("ma_loaded")
        mb_loaded = sem("mb_loaded")
        st_done = sem("st_done")
        exp_done = sem("exp_done")
        v_done = sem("v_done")
        v_taken = sem("v_taken")
        pv_done = sem("pv_done")
        ot_taken = sem("ot_taken")
        den_loaded = sem("den_loaded")
        rec_done = sem("rec_done")
        rec_written = sem("rec_written")
        rec_loaded = sem("rec_loaded")
        at_done = sem("at_done")
        ah_done = sem("ah_done")
        al_done = sem("al_done")
        xr_loaded = sem("xr_loaded")
        xb_done = sem("xb_done")
        o_done = sem("o_done")
        y_done = sem("y_done")
        y_stored = sem("y_stored")
        stats2_done = sem("stats2_done")
        mv2_done = sem("mv2_done")
        ve2_done = sem("ve2_done")
        rstd2_done = sem("rstd2_done")
        ln_done = sem("ln_done")
        ln_stored = sem("ln_stored")
        lmax_tmp = sem("lmax_tmp")
        lmax_done = sem("lmax_done")
        counts = {e.engine: e.alloc_register("count") for e in (nc.gpsimd, nc.sync, nc.scalar, nc.vector)}

        def count(n):
            return max(n, 0) if isinstance(n, int) else n

        def held(eng, n):
            if isinstance(n, int):
                return max(n, 0)
            eng.reg_mov(counts[eng.engine], n)
            eng.wait_ge(ident_set, 1)
            return counts[eng.engine]

        def upto(it, k):
            return min(max(it + k + 1, 0), NB) if isinstance(it, int) else it + (k + 1)

        def has(it, k):
            return not isinstance(it, int) or 0 <= it + k < NB

        def first(it, at):
            return isinstance(it, int) and it == at

        def iterations(eng, body):
            for it in SPAN:
                if it < FIRST:
                    body(it, it % 3)
            with eng.Fori(FIRST, LAST - 1, 3) as i:
                for d in range(3):
                    body(i + d, (FIRST + d) % 3)
            for it in SPAN:
                if it > LAST:
                    body(it, it % 3)

        block = es.enter_context(nc.Block())

        @block.sync
        def _(sp):
            sp.dma_start(xt[:, 0], xv[0]).then_inc(x_loaded, 16)
            for n in "qkv":
                sp.dma_start(wf[n], t["w" + n].rearrange("(t p) e -> p t e", p=P)).then_inc(w_loaded, 16)
            sp.dma_start(ct[:], cv[0]).then_inc(c_loaded, 16)
            sp.dma_start(gx[:], t["gx"].rearrange("(o d) -> o d", o=1).broadcast_to((P, 1))).then_inc(g_loaded, 16)
            sp.dma_start(gf[:], t["gf"].rearrange("(o d) -> o d", o=1).broadcast_to((P, 1))).then_inc(g_loaded, 16)
            sp.dma_start(bqk[:, 0, :], t["bq"]).then_inc(b_loaded, 16)
            sp.dma_start(bqk[:, 1, :], t["bk"]).then_inc(b_loaded, 16)
            sp.dma_start(bo[:], t["bo"].rearrange("(o d) -> o d", o=1).broadcast_to((P, D))).then_inc(b_loaded, 16)
            sp.wait_ge(wo_zeroed, 2)
            for c in range(4):
                h0 = 8 * (c // 2) + c % 2
                src = t["wo"].rearrange("(h j) n -> j h n", j=HD)[:, h0:h0 + 7:2, :]
                sp.dma_start(wof[32 * c:32 * c + HD, :, :], src).then_inc(wo_loaded, 16)
                sp.dma_start(bvc[32 * c:32 * c + HD, :], t["bv"][c * HD:(c + 1) * HD, :]).then_inc(wo_loaded, 16)

            def load_weights(i):
                name, cols = (("w_gate", D), ("w_up", D), ("w_down", F))[i]
                sp.dma_start(wn[i].rearrange("p (f d) -> p f d", d=cols),
                             t[name].rearrange("(f p) d -> p f d", p=P)).then_inc(wn_loaded, 16)

            def body(it, b):
                n = (b + 2) % 3
                if first(it, NB - 4):
                    sp.wait_ge(weights_split, 8)
                    load_weights(0)
                if first(it, NB - 2):
                    sp.wait_ge(xn_ready, NB)
                    sp.wait_ge(wn_loaded, 16)
                    load_weights(1)
                if has(it, -1):
                    sp.wait_ge(xb_done, held(sp, upto(it, -2)))
                    sp.dma_start(xr[:], xv[it - 1]).then_inc(xr_loaded, 16)
                if has(it, 4):
                    sp.wait_ge(xn_ready, held(sp, upto(it, 1)))
                    sp.wait_ge(x_loaded, held(sp, 16 * upto(it, 3)))
                    sp.dma_start(xt[:, (b + 1) % 3], xv[it + 4]).then_inc(x_loaded, 16)
                if has(it, -1):
                    sp.wait_ge(ot_taken, held(sp, 2 * upto(it, -1)))
                    sp.wait_ge(rec_done, held(sp, upto(it, -2)))
                    sp.dma_start(den[:], ot[HD:P:32, n].rearrange("p u q -> p (u q)")).then_inc(den_loaded, 16)
                if has(it, -2):
                    sp.wait_ge(y_done, held(sp, upto(it, -2)))
                    sp.dma_start(ov[it - 2], y[:]).then_inc(y_stored, 16)
                if has(it, 0):
                    sp.wait_ge(mh_done, held(sp, 2 * it + 2))
                    for r in range(2):
                        sp.dma_start(qst[96:97, b, r, 4:8, :], mrow[4 * r:4 * r + 4, 1, :]).then_inc(mb_loaded, 16)
                if has(it, -1):
                    sp.wait_ge(rec_done, held(sp, upto(it, -1)))
                    sp.dma_start(rec_dram[n].rearrange("c (g w) -> (c g) w", w=32), rec[:]).then_inc(rec_written, 16)
                if has(it, 3) and not first(it, -3):
                    sp.wait_ge(ct_done, held(sp, upto(it, 2)))
                    sp.dma_start(ct[:], cv[it + 3]).then_inc(c_loaded, 16)
                if has(it, -1):
                    sp.wait_ge(rec_written, held(sp, 16 * upto(it, -1)))
                    sp.wait_ge(at_done, held(sp, upto(it, -2)))
                    sp.dma_start(recb[:].rearrange("p u q -> p (u q)"),
                                 rec_dram[n].rearrange("c (o w) -> c o w", o=1).broadcast_to((4, 32, 4 * S))
                                 ).then_inc(rec_loaded, 16)
                kd = kst[:, n].rearrange("p j q -> p (j q)")
                qd = [qst[:, n, r].rearrange("p j q -> p (j q)") for r in range(2)]
                if has(it, 2):
                    sp.wait_ge(stack_loaded, held(sp, 128 * upto(it, -1)))
                    for i, (ready, written) in enumerate(((qh_done, q_written), (ql_done, q_written), (kh_done, k_written), (kl_done, k_written))):
                        sp.wait_ge(ready, held(sp, upto(it, 2)))
                        sp.dma_start(qk_dram[n, i].rearrange("r j (a c) -> a (r j) c", a=4),
                                     qk[:, i].rearrange("p t q -> p (t q)")).then_inc(written, 16)
                    sp.wait_ge(st_done, held(sp, UNITS * upto(it, -1)))
                    sp.wait_ge(q_written, held(sp, 32 * upto(it, 2)))
                    if first(it, -2):
                        sp.wait_ge(consts_set, 6)
                    for r in range(2):
                        lo = 48 * r
                        sp.dma_start(qd[r][lo:lo + 2 * HD], qk_dram[n, 0:1, r].broadcast_to((2, HD, 4 * KT * S))
                                     ).then_inc(stack_loaded, 16)
                        sp.dma_start(qd[r][lo + 2 * HD:lo + 3 * HD], qk_dram[n, 1, r]).then_inc(stack_loaded, 16)
                if has(it, 1):
                    sp.wait_ge(mh_done, held(sp, 2 * it + 3))
                    for r in range(2):
                        sp.dma_start(qst[96:97, (b + 1) % 3, r, 0:4, :], mrow[4 * r:4 * r + 4, 0, :]).then_inc(ma_loaded, 16)
                if has(it, 2):
                    sp.wait_ge(k_written, held(sp, 32 * upto(it, 2)))
                    for r in range(2):
                        lo = 48 * r
                        sp.dma_start(kd[lo:lo + 2 * HD], qk_dram[n, 2:4, r]).then_inc(stack_loaded, 16)
                        sp.dma_start(kd[lo + 2 * HD:lo + 3 * HD], qk_dram[n, 2, r]).then_inc(stack_loaded, 16)

                if has(it, -2):
                    sp.wait_ge(ln_done, held(sp, KT * upto(it, -2)))
                    sp.dma_start(t["lnall"][:, it - 2, :], ln[:].rearrange("p t d -> p (t d)")).then_inc(ln_stored, 16)
                if first(it, NB - 1):
                    sp.wait_ge(w_low, 1)
                    load_weights(2)

            iterations(nc.sync, body)
            sp.wait_ge(y_stored, 16 * NB)
            sp.wait_ge(ln_stored, 16 * NB)

        @block.tensor
        def _(pe):
            def split_product(o, lh, ll, rh, rl, last):
                terms = [(l, r, k) for l, r in ((lh, rh), (lh, rl), (ll, rh)) for k in range(last)]
                for n, (l, r, k) in enumerate(terms):
                    mm = nc.tensor.matmul(o, l(k), r(k), start=n == 0, stop=n == len(terms) - 1)
                return mm

            def project(bank, nm, xh_, xl_, done):
                for e in range(2):
                    mm = split_product(bank[:, e, :], lambda k: wh[nm][:, k, e * P:(e + 1) * P],
                                       lambda k: wl[nm][:, k, e * P:(e + 1) * P],
                                       lambda k: xh_[:, k, :], lambda k: xl_[:, k, :], 2)
                mm.then_inc(done, 1)

            def turn(bank, src, done):
                for d in range(2):
                    for tt in range(KT):
                        mm = nc.tensor.transpose(bank[:, d, tt * P:(tt + 1) * P], src[:, tt, d * P:(d + 1) * P], ident[:])
                mm.then_inc(done, 1)

            def turn_max(bank, b, hf):
                for tt in range(KT):
                    mm = nc.tensor.transpose(bank[0:8, 0, tt * P:(tt + 1) * P],
                                             negm[:, b, tt, 8 * hf:8 * hf + 8], ident[:])
                mm.then_inc(mt_done, 1)

            def turn_weights(k):
                i, part, half_ = k // 4, k % 4 // 2, k % 2
                pe.wait_ge(w_high, i + 1)
                pe.wait_ge(w_low, i + 1)
                pe.wait_ge(w_kept, max(k - 1, 0))
                bank = s_ps[k % 2][:].rearrange("p a b -> p (a b)").bitcast(F16)
                for f in range(6):
                    if i < 2:
                        at0 = f * D + half_ * P
                    else:
                        at0 = f % 2 * F + (3 * half_ + f // 2) * P
                    mm = nc.tensor.transpose(bank[:, f * P:(f + 1) * P], wq[:, i % 2, part, at0:at0 + P], t["ident16"][:])
                mm.then_inc(w_turned, 1)

            def values(bat, b, u):
                pe.wait_ge(exp_done, count(UNITS * bat + 2 * KT * (u + 1)))
                if u % 2 == 0:
                    pe.wait_ge(ot_taken, count(2 * bat + u // 2))
                for kt in range(KT):
                    for c in range(4):
                        mm = nc.tensor.matmul(pv_ps[32 * c:32 * c + 32, u % 2, :],
                                              vt[:, b, kt, 8 * (c // 2) + 2 * u + c % 2, :],
                                              pt[:, u % 2, c // 2, kt, c % 2, :],
                                              start=kt == 0, stop=kt == KT - 1)
                mm.then_inc(pv_done, 1)

            pe.wait_ge(bv_spread, 1)
            pe.wait_ge(wo_loaded, 128)
            for u in range(4):
                mm = nc.tensor.matmul(misc[1][:, 0, :], bvw[:, u, :], wof[:, u, :], start=u == 0, stop=u == 3)
            mm.then_inc(bvo_done, 1)
            pe.wait_ge(ident_set, 2)
            pe.wait_ge(weights_split, 8)
            pe.wait_ge(gate_scaled, 3)

            def body(it, b):
                for j in range(PAIRS):
                    bank = misc[j % 2]
                    if j == 0 and has(it, 2):
                        pe.wait_ge(v_taken, upto(it, 1))
                        pe.wait_ge(xn_ready, upto(it, 2))
                        turn(bank, xn, xt_done)
                    if j == 1 and has(it, 0):
                        pe.wait_ge(y_done, upto(it, -2))
                        pe.wait_ge(max_done, 16 * upto(it, 0))
                        turn_max(bank, b, 1)
                    if j == 2 and has(it, 2):
                        pe.wait_ge(xl_done, upto(it, 2))
                        pe.wait_ge(c_loaded, 16 * upto(it, 2))
                        turn(bank, ct, ct_done)
                    if j == 3 and has(it, 2):
                        pe.wait_ge(mh_done, 2 * upto(it, 0))
                        pe.wait_ge(xl_done, upto(it, 2))
                        project(bank, "q", xh, xl, q_done)
                    if j == 4 and has(it, 2):
                        pe.wait_ge(cl_done, upto(it, 2))
                        project(bank, "k", ch, cl, k_done)
                    if j == 5 and has(it, 1):
                        pe.wait_ge(ql_done, upto(it, 2))
                        pe.wait_ge(qh_done, upto(it, 2))
                        pe.wait_ge(mh_done, 2 * upto(it, 0))
                        pe.wait_ge(max_done, count(16 * (it + 1) + 8))
                        turn_max(bank, (b + 1) % 3, 0)
                    if j == 6 and has(it, 2):
                        pe.wait_ge(kl_done, upto(it, 2))
                        pe.wait_ge(kh_done, upto(it, 2))
                        for tt in range(KT):
                            mm = split_product(bank[:, tt, :], lambda k: ch[:, k, tt * P:(tt + 1) * P],
                                               lambda k: cl[:, k, tt * P:(tt + 1) * P],
                                               lambda k: wh["v"][:, k, :], lambda k: wl["v"][:, k, :], 2)
                        mm.then_inc(v_done, 1)
                    if j == 7 and has(it, -1):
                        pe.wait_ge(mh_done, count(2 * it + 3) if has(it, 1) else 2 * NB)
                        pe.wait_ge(y_done, upto(it, -2))
                        pe.wait_ge(al_done, upto(it, -1))
                        pe.wait_ge(ah_done, upto(it, -1))
                        for tt in range(KT):
                            mm = split_product(bank[:, tt, :], lambda k: ah[:, k, tt * P:(tt + 1) * P],
                                               lambda k: al[:, k, tt * P:(tt + 1) * P],
                                               lambda k: woh[:, k, :], lambda k: wol[:, k, :], 4)
                        mm.then_inc(o_done, 1)

                    if has(it, 1):
                        n = (b + 1) % 3
                        if j == 0:
                            pe.wait_ge(stack_loaded, 128 * upto(it, 1))
                        for tt in range(KT):
                            pe.wait_ge(max_done, count(16 * (it + 1) + 2 * j + tt - 1))
                            for r in range(2):
                                mm = nc.tensor.matmul(s_ps[tt][:, r, :], qst[0:96, n, r, j, tt * P:(tt + 1) * P],
                                                      kst[0:96, n, j, :], start=True, stop=True)
                            mm.then_inc(s_done, 1)
                    if j == 0 and has(it, -1):
                        values(it - 1, (b + 2) % 3, 3)
                    if has(it, 0):
                        if j == 0:
                            pe.wait_ge(ma_loaded, count(32 * it + 32))
                        if j == 4:
                            pe.wait_ge(mb_loaded, count(32 * it + 32))
                        for kt in range(KT):
                            u = KT * j + kt
                            pe.wait_ge(exp_done, count(UNITS * it + u - 2))
                            nc.tensor.matmul(st_ps[(b + u) % 3][:], kst[:, b, j, kt * P:(kt + 1) * P],
                                             qst[:, b, :, j, :], start=True, stop=True).then_inc(st_done, 1)
                    if first(it, NB) and 1 <= j <= 4:
                        if j == 1:
                            pe.wait_ge(ident16_set, 1)
                            pe.wait_ge(max_done, 16 * NB)
                        turn_weights(j - 1)
                    if first(it, NB + 1):
                        turn_weights(4 + j)
                    if j in (2, 4, 6) and has(it, 0):
                        if j == 2:
                            pe.wait_ge(v_taken, count(it + 1))
                        values(it, b, j // 2 - 1)

            iterations(nc.tensor, body)

        @block.scalar
        def _(act):
            act.wait_ge(g_loaded, 32)
            nc.scalar.activation(tg[:], gx[:], ACT.Tanh).then_inc(gate_done, 1)
            nc.scalar.activation(t["tgf"][:], gf[:], ACT.Tanh).then_inc(gate_done, 1)
            act.wait_ge(w_loaded, 48)
            for n in "qkv":
                nc.scalar.activation(wh[n][:], wf[n], ACT.Copy, scale=WS).then_inc(weights_split, 1)
            act.wait_ge(wo_loaded, 128)
            nc.scalar.activation(woh[:], wof[:], ACT.Copy, scale=WS).then_inc(weights_split, 1)
            act.wait_ge(bias_ready, 1)

            def take(bat, b, hf):
                act.wait_ge(pv_done, count(4 * bat + 2 * hf + 2))
                act.wait_ge(at_done, count(bat - 1))
                nc.scalar.copy(ot[:, b, 2 * hf:2 * hf + 2, :], pv_ps[:]).then_inc(ot_taken, 1)

            def max_row(bat, hf):
                act.wait_ge(mt_done, count(2 * bat + hf + 1))
                act.wait_ge((ma_loaded, mb_loaded)[hf], count(32 * bat))
                nc.scalar.activation(mrow[:, hf, :], misc[1][0:8, 0, :], ACT.Copy, scale=1.0 / MS).then_inc(mh_done, 1)

            def high_weights(i):
                act.wait_ge(w_real, i + 1)
                if i == 2:
                    act.wait_ge(w_turned, 4)
                nc.scalar.copy(wq[:, i % 2, 0], wn[i]).then_inc(w_high, 1)

            def keep_weights(k):
                act.wait_ge(w_turned, k + 1)
                i, part, half_ = k // 4, k % 4 // 2, k % 2
                bank = s_ps[k % 2][:].rearrange("p a b -> p (a b)").bitcast(F16)[:, 0:F]
                if i < 2:
                    dst = t[("wgt", "wut")[i]][:, part, half_]
                else:
                    dst = t["wdt"][:, part, 3 * half_:3 * half_ + 3].rearrange("p f d -> p (f d)")
                nc.scalar.copy(dst, bank).then_inc(w_kept, 1)

            def high(i, bank, done):
                for e in range(2):
                    op = nc.scalar.activation(qk[:, 2 * i, e, :], bank[:, e, :], ACT.Identity, bias=bqk_s[:, i, e:e + 1])
                op.then_inc(done, 1)

            def body(it, b):
                for j in range(PAIRS):
                    if j == 0 and has(it, 2):
                        act.wait_ge(xt_done, upto(it, 2))
                        act.wait_ge(q_done, upto(it, 1))
                        nc.scalar.copy(xh[:], misc[0][:]).then_inc(xh_done, 1)
                    if j == 1 and has(it, 0):
                        max_row(it, 1)
                    if j == 2 and has(it, 2):
                        act.wait_ge(ct_done, upto(it, 2))
                        act.wait_ge(v_done, upto(it, 1))
                        nc.scalar.copy(ch[:], misc[0][:]).then_inc(ch_done, 1)
                    if j == 3 and has(it, 2):
                        act.wait_ge(q_done, upto(it, 2))
                        act.wait_ge(q_written, 32 * upto(it, 1))
                        high(0, misc[1], qh_done)
                    if j == 4 and has(it, 2):
                        act.wait_ge(k_done, upto(it, 2))
                        act.wait_ge(k_written, 32 * upto(it, 1))
                        high(1, misc[0], kh_done)
                    if j == 5 and has(it, 1):
                        max_row(it + 1, 0)
                    if j == 6 and has(it, -1):
                        act.wait_ge(at_done, upto(it, -1))
                        act.wait_ge(o_done, upto(it, -2))
                        nc.scalar.copy(ah[:], at[:]).then_inc(ah_done, 1)
                    if j == 7 and has(it, 2):
                        act.wait_ge(v_done, upto(it, 2))
                        act.wait_ge(pv_done, 4 * upto(it, -1))
                        nc.scalar.activation(vt[:, (b + 2) % 3, :, :, 0:HD], misc[0][:].rearrange("p t (h j) -> p t h j", j=HD),
                                             ACT.Copy, scale=1.0 / WS).then_inc(v_taken, 1)
                    if j == 0 and has(it, -1):
                        take(it - 1, (b + 2) % 3, 1)
                    if has(it, 0):
                        act.wait_ge(pv_done, count(4 * it + j // 2 - 1))
                        for kt in range(KT):
                            u = KT * j + kt
                            act.wait_ge(st_done, count(UNITS * it + u + 1))
                            nc.scalar.activation(pt[:, (j // 2) % 2, j % 2, kt], st_ps[(b + u) % 3][:], ACT.Exp,
                                                 scale=1.0 / (WS * WS * HD ** 0.5)).then_inc(exp_done, 1)
                    if first(it, NB - 1) and j == 3:
                        high_weights(0)
                    if first(it, NB - 1) and j == 7:
                        high_weights(1)
                    if first(it, NB) and 1 <= j <= 4:
                        keep_weights(j - 1)
                    if first(it, NB) and j == 7:
                        high_weights(2)
                    if first(it, NB + 1):
                        keep_weights(4 + j)
                    if j == 4 and has(it, 0):
                        take(it, b, 0)

            iterations(nc.scalar, body)

        @block.vector
        def _(dve):
            def normal_stats(bat, b):
                dve.wait_ge(x_loaded, 16 * (bat + 1))
                for tt in range(KT):
                    nc.vector.bn_stats(stats[:, tt, :], xt[:, b, tt, :]).then_inc(stats_done, 1)
                dve.wait_ge(xn_ready, bat)
                dve.wait_ge(stats_done, held(dve, KT * (bat + 1)))
                for tt in range(KT):
                    nc.vector.bn_aggr(mv[:, tt, :], stats[:, tt, :]).then_inc(mv_done, 1)

            nc.vector.memset(half[:], -0.5).then_inc(consts_set, 1)
            nc.vector.memset(wof[:], 0.0).then_inc(wo_zeroed, 1)
            nc.vector.memset(bvc[:], 0.0).then_inc(wo_zeroed, 1)
            nc.vector.memset(lmax[:], 0.0).then_inc(lmax_done, 1)
            nc.vector.memset(kst[96:97], MS).then_inc(consts_set, 1)
            normal_stats(0, 0)
            dve.wait_ge(weights_split, 3)
            for n in "qkv":
                nc.vector.scalar_tensor_tensor(out=wl[n][:], in0=wf[n], scalar=WS, in1=wh[n][:], op0=ALU.mult,
                                               op1=ALU.subtract).then_inc(weights_split, 1)
            dve.wait_ge(wo_loaded, 128)
            nc.vector.tensor_copy(bvw, bvc[:].rearrange("p (u o) -> p u o", o=1).broadcast_to((P, 4, P))).then_inc(bv_spread, 1)
            dve.wait_ge(weights_split, 7)
            nc.vector.scalar_tensor_tensor(out=wol[:], in0=wof[:], scalar=WS, in1=woh[:], op0=ALU.mult,
                                           op1=ALU.subtract).then_inc(weights_split, 1)
            dve.wait_ge(b_loaded, 48)
            nc.vector.tensor_scalar(bqk_s[:], bqk[:], WS, None, ALU.mult).then_inc(bias_ready, 1)
            dve.wait_ge(gate_done, 1)
            nc.vector.tensor_scalar(tgs[:], tg[:], 1.0 / WS, None, ALU.mult).then_inc(gate_scaled, 1)
            dve.wait_ge(bvo_done, 1)
            nc.vector.tensor_tensor(tbo[:], misc[1][:, 0, :], bo[:], ALU.add).then_inc(gate_scaled, 1)
            dve.wait_ge(gate_scaled, 2)
            nc.vector.tensor_scalar(tbo[:], tbo[:], tg[:, 0:1], None, ALU.mult).then_inc(gate_scaled, 1)
            dve.wait_ge(bias_ready, 1)
            dve.wait_ge(ident_set, 2)
            nc.vector.tensor_copy(t["ident16"][:], ident[:]).then_inc(ident16_set, 1)

            def blocks(a):
                return a.rearrange("p (k w) -> p k w", w=BLOCK)

            def wide(a):
                return a[:].rearrange("p (k o) -> p k o", o=1).broadcast_to((P, NBLK, BLOCK))

            def block_scales(i):
                dve.wait_ge(wn_loaded, 16 * (i + 1))
                nc.vector.tensor_reduce(bm[:], blocks(wn[i]), AX.X, ALU.max, apply_absolute_value=True).then_inc(blk_max, 1)
                dve.wait_ge(blk_max, i + 1)
                nc.vector.tensor_scalar(bs[:], bm[:], 1.0 / 7.0, 1e-12, ALU.mult, ALU.max).then_inc(blk_scaled, 1)
                dve.wait_ge(blk_scaled, 2 * i + 1)
                nc.vector.reciprocal(bi[:], bs[:]).then_inc(blk_inv, 1)
                nc.vector.tensor_scalar(bf[:], bs[:], FS, None, ALU.mult).then_inc(blk_scaled, 1)

            def to_integers(i):
                dve.wait_ge(blk_inv, i + 1)
                nc.vector.tensor_tensor(blocks(wi[:]), blocks(wn[i]), wide(bi), ALU.mult).then_inc(w_int, 1)
                dve.wait_ge(w_int, i + 1)
                nc.vector.tensor_scalar(wi[:], wi[:], 7.0, -8.0, ALU.min, ALU.max).then_inc(w_clipped, 1)

            def from_integers(i):
                dve.wait_ge(w_clipped, i + 1)
                dve.wait_ge(blk_scaled, 2 * i + 2)
                nc.vector.tensor_tensor(blocks(wn[i]), blocks(wi[:]), wide(bf), ALU.mult).then_inc(w_real, 1)

            def quantise(i):
                block_scales(i)
                to_integers(i)
                from_integers(i)

            def low_weights(i):
                dve.wait_ge(w_high, i + 1)
                nc.vector.tensor_tensor(wq[:, i % 2, 1], wn[i], wq[:, i % 2, 0], ALU.subtract).then_inc(w_low, 1)

            def low(i, bank, done):
                for e in range(2):
                    op = nc.vector.scalar_tensor_tensor(out=qk[:, 2 * i + 1, e, :], in0=bank[:, e, :],
                                                        scalar=bqk_s[:, i, e:e + 1], in1=qk[:, 2 * i, e, :],
                                                        op0=ALU.add, op1=ALU.subtract)
                op.then_inc(done, 1)

            def body(it, b):
                def row_maxima(j, tt):
                    if has(it, 1):
                        dve.wait_ge(s_done, count(16 * (it + 1) + 2 * j + tt + 1))
                        lo = 8 * (j // 4) + j % 4
                        nc.vector.tensor_reduce(negm[:, (b + 1) % 3, tt, lo:lo + 5:4], s_ps[tt][:], AX.X, ALU.max,
                                                negate=True).then_inc(max_done, 1)

                for j in range(PAIRS):
                    if j == 7 and has(it, -2):
                        if first(it, NB + 1):
                            dve.wait_ge(rstd2_done, NB)
                            dve.wait_ge(ln_stored, 16 * (NB - 1))
                            for tt in range(KT):
                                nc.vector.tensor_scalar(ln[:, tt, :], y[:, tt, :], mv2[:, tt, 0:1], rstd2[:, tt:tt + 1],
                                                        ALU.subtract, ALU.mult).then_inc(ln_done, 1)
                        dve.wait_ge(ln_done, KT * upto(it, -2))
                        dve.wait_ge(lmax_done, upto(it, -2))
                        nc.vector.tensor_reduce(t["lnmax"][:], ln[:], AX.XY, ALU.max,
                                                apply_absolute_value=True).then_inc(lmax_tmp, 1)
                        dve.wait_ge(lmax_tmp, upto(it, -2))
                        nc.vector.tensor_tensor(lmax[:], lmax[:], t["lnmax"][:], ALU.max).then_inc(lmax_done, 1)
                    row_maxima(j, 0)
                    if j == 6 and has(it, -1):
                        dve.wait_ge(ah_done, upto(it, -1))
                        dve.wait_ge(o_done, upto(it, -2))
                        nc.vector.tensor_tensor(al[:], at[:], ah[:], ALU.subtract).then_inc(al_done, 1)
                    if j == 2 and has(it, -1):
                        dve.wait_ge(den_loaded, 16 * upto(it, -1))
                        dve.wait_ge(rec_written, 16 * upto(it, -2))
                        nc.vector.reciprocal(rec[:], den[:]).then_inc(rec_done, 1)
                    if j == 3 and has(it, 2):
                        dve.wait_ge(qh_done, upto(it, 2))
                        low(0, misc[1], ql_done)
                    if j == 4 and has(it, 2):
                        dve.wait_ge(kh_done, upto(it, 2))
                        low(1, misc[0], kl_done)
                    if j == 5 and has(it, 4):
                        normal_stats(it + 4, (b + 1) % 3)
                    row_maxima(j, 1)
                    if j == 0 and has(it, 2):
                        dve.wait_ge(xh_done, upto(it, 2))
                        nc.vector.tensor_tensor(xl[:], misc[0][:], xh[:], ALU.subtract).then_inc(xl_done, 1)
                    if j == 2 and has(it, 2):
                        dve.wait_ge(ch_done, upto(it, 2))
                        nc.vector.tensor_tensor(cl[:], misc[0][:], ch[:], ALU.subtract).then_inc(cl_done, 1)
                    if j == 2 and has(it, -2):
                        dve.wait_ge(y_done, upto(it, -2))
                        dve.wait_ge(ln_done, KT * upto(it, -3))
                        for tt in range(KT):
                            nc.vector.bn_stats(stats2[:, tt, :], y[:, tt, :]).then_inc(stats2_done, 1)
                        dve.wait_ge(stats2_done, held(dve, KT * upto(it, -2)))
                        for tt in range(KT):
                            nc.vector.bn_aggr(mv2[:, tt, :], stats2[:, tt, :]).then_inc(mv2_done, 1)
                    if first(it, NB - 4) and j == 6:
                        block_scales(0)
                    if first(it, NB - 3) and j == 6:
                        to_integers(0)
                    if first(it, NB - 2) and j == 6:
                        from_integers(0)
                    if first(it, NB - 1) and j == 2:
                        quantise(1)
                        low_weights(0)
                    if first(it, NB) and j == 2:
                        quantise(2)
                        low_weights(1)
                    if first(it, NB) and j == 7:
                        low_weights(2)
                    if j == 7 and has(it, -1):
                        dve.wait_ge(o_done, upto(it, -1))
                        dve.wait_ge(xb_done, upto(it, -1))
                        dve.wait_ge(y_stored, 16 * upto(it, -2))
                        dve.wait_ge(ln_done, KT * upto(it, -2))
                        nc.vector.scalar_tensor_tensor(out=y[:], in0=misc[1][:], scalar=tgs[:, 0:1], in1=xb[:],
                                                       op0=ALU.mult, op1=ALU.add).then_inc(y_done, 1)


            iterations(nc.vector, body)

        @block.gpsimd
        def _(pool):
            nc.gpsimd.memset(ident[:], 0.0).then_inc(ident_set, 1)
            pool.wait_ge(ident_set, 1)
            nc.gpsimd.affine_select(out=ident[:], in_=ident[:], compare_op=ALU.not_equal, fill=1.0, base=0,
                                    pattern=[[-1, P]], channel_multiplier=1).then_inc(ident_set, 1)
            nc.gpsimd.memset(vt[:, :, :, :, HD:32], 0.0).then_inc(ident_set, 1)
            pool.wait_ge(ident_set, 3)
            nc.gpsimd.memset(vt[:, :, :, :, HD:HD + 1], 1.0).then_inc(consts_set, 1)
            pool.wait_ge(consts_set, 3)

            def root(var, eps_out, out_, first, second, batches):
                nc.gpsimd.tensor_scalar(eps_out[:], var, EPS, 1.0, ALU.add, ALU.mult).then_inc(first, 1)
                pool.wait_ge(first, held(pool, batches))
                nc.gpsimd.tensor_tensor(out_[:], eps_out[:], half[:], ALU.pow).then_inc(second, 1)

            def body(it, b):
                n = (b + 2) % 3
                if has(it, 3):
                    pool.wait_ge(mv_done, held(pool, KT * upto(it, 3)))
                    root(mv[:, :, 1], ve, rstd, ve_done, rstd_done, upto(it, 3))
                    pool.wait_ge(rstd_done, held(pool, upto(it, 3)))
                    pool.wait_ge(xt_done, held(pool, upto(it, 2)))
                    for tt in range(KT):
                        op = nc.gpsimd.tensor_scalar(xn[:, tt, :], xt[:, b, tt, :], mv[:, tt, 0:1],
                                                     rstd[:, tt:tt + 1], ALU.subtract, ALU.mult)
                    op.then_inc(xn_ready, 1)
                if has(it, -1):
                    if first(it, 1):
                        pool.wait_ge(gate_scaled, 3)
                    pool.wait_ge(xr_loaded, held(pool, 16 * upto(it, -1)))
                    pool.wait_ge(y_done, held(pool, upto(it, -2)))
                    nc.gpsimd.tensor_tensor(xb[:], xr[:], tbo[:].rearrange("p (o d) -> p o d", o=1).broadcast_to((P, KT, D)),
                                            ALU.add).then_inc(xb_done, 1)
                if has(it, -1):
                    pool.wait_ge(rec_loaded, held(pool, 16 * upto(it, -1)))
                    pool.wait_ge(al_done, held(pool, upto(it, -2)))
                    nc.gpsimd.tensor_tensor(at[:], ot[:, n], recb[:], ALU.mult).then_inc(at_done, 1)
                if has(it, -2):
                    pool.wait_ge(mv2_done, held(pool, KT * upto(it, -2)))
                    root(mv2[:, :, 1], ve2, rstd2, ve2_done, rstd2_done, upto(it, -2))
                if has(it, -2) and not first(it, NB + 1):
                    pool.wait_ge(rstd2_done, held(pool, upto(it, -2)))
                    pool.wait_ge(lmax_tmp, held(pool, upto(it, -3)))
                    pool.wait_ge(ln_stored, held(pool, 16 * upto(it, -3)))
                    for tt in range(KT):
                        nc.gpsimd.tensor_scalar(ln[:, tt, :], y[:, tt, :], mv2[:, tt, 0:1], rstd2[:, tt:tt + 1],
                                                ALU.subtract, ALU.mult).then_inc(ln_done, 1)
                if first(it, -3):
                    for n in range(3):
                        nc.gpsimd.memset(qst[:, n], 0.0).then_inc(consts_set, 1)

            iterations(nc.gpsimd, body)
            pool.wait_ge(lmax_done, NB + 1)
            nc.gpsimd.partition_all_reduce(t["lmaxall"][:], lmax[:], P, RMAX).then_inc(lmax_tmp, 1)
            pool.wait_ge(lmax_tmp, NB + 1)


def feed_forward(nc, t, out):
    NB, S, D = out.shape
    F = t["w_gate"].shape[0]
    KT = S // P
    DT = D // P
    FT = F // P
    CB = 2
    CW = CB * S
    NC = NB // CB
    PR = FT // 2
    ov = out.rearrange("b (p t) d -> b p t d", t=KT)

    with ExitStack() as es:
        def sb(name, shape, dt):
            return es.enter_context(nc.sbuf_tensor(name, shape, dt))

        def sem(name):
            return es.enter_context(nc.semaphore(name))

        ident, wgt, wut, wdt = t["ident16"], t["wgt"], t["wut"], t["wdt"]
        xq = sb("xq", [P, 2, NC, DT, CW], F16)
        scal = sb("scal", [P, 16], F32)
        cmax = sb("cmax", [P, 4, NC * PR], F32)
        vmax = sb("vmax", [P, 4, 2], F32)
        gb = sb("gb", [P, NC, FT, CW], F32)
        h3 = sb("h3", [P, 2, FT, CW], F16)
        ps = es.enter_context(nc.psum_tensor("pairs", [P, 4, 2, CW], F32))
        xi = h3[:].rearrange("p d f w -> p (d f w)")[:, 0:2 * CB * KT * D].bitcast(I16).rearrange(
            "p (d b t e) -> p d b t e", d=2, b=CB, t=KT)
        words = t["lnall"]
        ia = words[:, 0:6, :].rearrange("p b c -> p (b c)").bitcast(I16).rearrange("p (d f w) -> p d f w", d=2, f=FT)
        ib = words[:, 6:12, :].rearrange("p b c -> p (b c)").bitcast(I16).rearrange("p (d f w) -> p d f w", d=2, f=FT)
        yb = words[:, 12:16, :].rearrange("p (d b) c -> p d b c", d=2)

        always = sem("f_always")
        x_int = sem("f_x_int")
        xt_turned = sem("f_xt_turned")
        xt_high = sem("f_xt_high")
        xt_low = sem("f_xt_low")
        chain = sem("f_chain")
        part_max = sem("f_part_max")
        all_max = sem("f_all_max")
        g_done = sem("f_g_done")
        g_kept = sem("f_g_kept")
        g_max = sem("f_g_max")
        qg_done = sem("f_qg_done")
        sig_done = sem("f_sig_done")
        sq_done = sem("f_sq_done")
        p2_done = sem("f_p2_done")
        p2_max = sem("f_p2_max")
        u_done = sem("f_u_done")
        u_max = sem("f_u_max")
        u2_done = sem("f_u2_done")
        qu_done = sem("f_qu_done")
        q2_done = sem("f_q2_done")
        p3_done = sem("f_p3_done")
        p3_max = sem("f_p3_max")
        q3_done = sem("f_q3_done")
        h3_done = sem("f_h3_done")
        l3_done = sem("f_l3_done")
        d_done = sem("f_d_done")
        z_done = sem("f_z_done")
        y_loaded = [sem(f"f_y_loaded{d}") for d in range(2)]
        z_stored = [sem(f"f_z_stored{d}") for d in range(2)]
        counts = {e.engine: e.alloc_register("count_ffn") for e in (nc.gpsimd, nc.sync, nc.scalar, nc.vector)}

        def held(eng, n):
            if isinstance(n, int):
                return n
            eng.reg_mov(counts[eng.engine], n)
            eng.wait_ge(always, 1)
            return counts[eng.engine]

        SX, KX, SG, KG, SU, KU, S2, K2, S3, K3, KD, TMP = range(12)

        def col(k):
            return scal[:, k:k + 1]

        def rounds(eng, first, last, body):
            with eng.Fori(first, last, 2) as i:
                for d in range(2):
                    body(i + d, d)

        def gate_rounds(eng, body):
            rounds(eng, 0, NC - 5, body)
            for c in range(NC - 4, NC):
                body(c, c % 2)

        def ahead(c, k):
            return not isinstance(c, int) or c + k < NC

        block = es.enter_context(nc.Block())

        @block.tensor
        def _(pe):
            def turn(c, d):
                pe.wait_ge(x_int, c + 1)
                bank = ps[:, 3, d].bitcast(F16)
                for e in range(DT):
                    for k in range(CB * KT):
                        mm = nc.tensor.transpose(bank[:, e * CW + k * P:e * CW + (k + 1) * P],
                                                 xi[:, d, k // KT, k % KT, e * P:(e + 1) * P].bitcast(F16), ident[:])
                mm.then_inc(xt_turned, 1)

            def products(w, c, p):
                for k in range(2):
                    f = 2 * p + k
                    terms = [(a, b, dt) for a, b in ((0, 0), (0, 1), (1, 0)) for dt in range(DT)]
                    for n, (a, b, dt) in enumerate(terms):
                        mm = nc.tensor.matmul(ps[:, p, k, :], w[:, a, dt, f * P:(f + 1) * P],
                                              xq[:, b, c, dt, :], start=n == 0, stop=n == len(terms) - 1)
                return mm

            turn(0, 0)
            turn(1, 1)

            def gate(c, d):
                pe.wait_ge(xt_low, c + 1)
                if ahead(c, 2):
                    turn(c + 2, d)
                for p in range(PR):
                    pe.wait_ge(g_kept, PR * c + p + 1)
                    products(wgt, c, p).then_inc(g_done, 1)
            gate_rounds(nc.tensor, gate)
            pe.wait_ge(g_kept, PR * NC + PR)

            def up(c, d):
                for p in range(PR):
                    pe.wait_ge(u_max, PR * c + p + 1)
                    products(wut, c, p).then_inc(u_done, 1)
            rounds(nc.tensor, 0, NC - 1, up)
            pe.wait_ge(u_max, PR * NC + PR)

            def up_again(c, d):
                for p in range(PR):
                    pe.wait_ge(qu_done, PR * c + p + 1)
                    products(wut, c, p).then_inc(u2_done, 1)
            rounds(nc.tensor, 0, NC - 1, up_again)

            def down(c, d):
                for b in range(CB):
                    pe.wait_ge(h3_done, CB * c + b + 1)
                    pe.wait_ge(z_done, CB * c + b + 1)
                    for tt in range(KT):
                        tok = (b * KT + tt) * P
                        terms = [(l, h, f) for l, h in ((0, 0), (0, 1), (1, 0)) for f in range(FT)]
                        for n, (l, h, f) in enumerate(terms):
                            src = (h3, ia)[l]
                            if l and tt == 0 and f == 0:
                                pe.wait_ge(l3_done, CB * c + b + 1 + 2 * CB)
                            lh = src[:, d, f, tok:tok + P]
                            if l:
                                lh = lh.bitcast(F16)
                            mm = nc.tensor.matmul(ps[:, 3, b, tt * D:(tt + 1) * D], lh, wdt[:, h, f, :],
                                                  start=n == 0, stop=n == len(terms) - 1)
                    mm.then_inc(d_done, 1)
            pe.sem_inc(d_done, 2 * CB)
            rounds(nc.tensor, 0, NC - 1, down)

        @block.scalar
        def _(act):
            act.sem_inc(g_kept, PR)
            act.sem_inc(qu_done, PR)

            def high(c, d):
                act.wait_ge(xt_turned, c + 1)
                nc.scalar.copy(xq[:, 0, c], ps[:, 3, d].bitcast(I16).rearrange("p (e w) -> p e w", e=DT)
                               ).then_inc(xt_high, 1)
            high(0, 0)

            def keep(c, d):
                if ahead(c, 1):
                    high(c + 1, 1 - d)
                for p in range(PR):
                    act.wait_ge(g_done, held(act, PR * c + p + 1))
                    nc.scalar.copy(gb[:, c, 2 * p:2 * p + 2, :], ps[:, p]).then_inc(g_kept, 1)
            gate_rounds(nc.scalar, keep)

            act.wait_ge(chain, 2 + 4)

            def gate_int(c, d):
                act.wait_ge(p2_done, PR * c + PR)
                nc.scalar.activation(ia[:, d], gb[:, c], ACT.Copy, scale=col(KG)).then_inc(qg_done, 1)

            def gate(c, d):
                act.wait_ge(qg_done, held(act, c + 1))
                nc.scalar.activation(gb[:, c], ia[:, d], ACT.Sigmoid, scale=col(SG)).then_inc(sig_done, 1)
                act.wait_ge(sig_done, held(act, c + 1))
                nc.scalar.activation(ib[:, d].bitcast(U16), gb[:, c], ACT.Copy, scale=LEVELS).then_inc(sq_done, 1)
                if ahead(c, 1):
                    gate_int(c + 1, 1 - d)
            gate_int(0, 0)
            rounds(nc.scalar, 0, NC - 3, gate)
            gate(NC - 2, 0)
            gate(NC - 1, 1)

            def up_integers(c, d):
                for p in range(PR):
                    act.wait_ge(u2_done, PR * c + p + 1)
                    nc.scalar.activation(ia[:, d, 2 * p:2 * p + 2, :], ps[:, p], ACT.Copy, scale=col(KU)
                                         ).then_inc(qu_done, 1)

            def gate_integers(c, d):
                nc.scalar.activation(ib[:, d], gb[:, c], ACT.Copy, scale=col(K2)).then_inc(q2_done, 1)

            act.wait_ge(chain, 2 + 4 + 4)
            for d in range(2):
                act.wait_ge(p2_done, PR * (NC - 1 + d) + 2 * PR)
                up_integers(d, d)
            act.wait_ge(chain, 2 + 4 + 4 + 4)
            for d in range(2):
                gate_integers(d, d)

            def integers(c, d):
                act.wait_ge(p3_done, PR * c - PR)
                gate_integers(c, d)
                up_integers(c, d)
            rounds(nc.scalar, 2, NC - 1, integers)

            act.wait_ge(chain, 2 + 4 + 4 + 4 + 4)

            def last(c, d):
                for b in range(CB):
                    tok = slice(b * S, (b + 1) * S)
                    act.wait_ge(l3_done, CB * c + b + 1)
                    nc.scalar.activation(ib[:, d, :, tok], gb[:, c, :, tok], ACT.Copy, scale=col(K3)).then_inc(q3_done, 1)
                    act.wait_ge(q3_done, held(act, CB * c + b + 1))
                    act.wait_ge(d_done, held(act, CB * c + b + 1))
                    nc.scalar.copy(h3[:, d, :, tok], ib[:, d, :, tok]).then_inc(h3_done, 1)
            rounds(nc.scalar, 0, NC - 1, last)

        @block.vector
        def _(dve):
            links = [0]

            def linked(op):
                op.then_inc(chain, 1)
                links[0] += 1
                dve.wait_ge(chain, links[0])

            def scale(m, unit, imm, s, k):
                linked(nc.vector.tensor_scalar(col(TMP), m, unit, imm / QMAX, ALU.mult, ALU.mult))
                linked(nc.vector.tensor_scalar(col(s), col(TMP), 1e-12, None, ALU.max))
                linked(nc.vector.reciprocal(col(TMP), col(s)))
                linked(nc.vector.tensor_scalar(col(k), col(TMP), unit, imm, ALU.mult, ALU.mult))

            dve.sem_inc(u_max, PR)
            dve.sem_inc(p2_done, 2 * PR)
            dve.sem_inc(l3_done, 2 * CB)
            dve.sem_inc(z_done, CB)
            dve.sem_inc(always, 1)
            linked(nc.vector.tensor_scalar(col(SX), t["lmaxall"][:], 1.0 / QMAX, 1e-12, ALU.mult, ALU.max))
            linked(nc.vector.reciprocal(col(KX), col(SX)))

            def integers(c, d):
                nc.vector.tensor_scalar(xi[:, d].rearrange("p b t e -> p b (t e)"), words[:, bass.ds(CB * c, CB)],
                                        col(KX), None, ALU.mult).then_inc(x_int, 1)

            def low(c, d):
                dve.wait_ge(xt_high, c + 1)
                nc.vector.tensor_tensor(xq[:, 1, c], ps[:, 3, d].bitcast(I16).rearrange("p (e w) -> p e w", e=DT),
                                        xq[:, 0, c], ALU.subtract).then_inc(xt_low, 1)

            def whole(i, width):
                nc.vector.tensor_reduce(vmax[:, i, 0:1], cmax[:, i, 0:width], AX.X, ALU.max).then_inc(part_max, 1)

            integers(0, 0)
            integers(1, 1)
            low(0, 0)
            dve.wait_ge(xt_turned, 1)
            integers(2, 0)

            def gate_max(c, d):
                if ahead(c, 1):
                    low(c + 1, 1 - d)
                if ahead(c, 3):
                    dve.wait_ge(xt_turned, c + 2)
                    integers(c + 3, 1 - d)
                dve.wait_ge(g_kept, PR * c + PR + PR)
                nc.vector.tensor_reduce(cmax[:, 0, bass.ds(c, 1)], gb[:, c], AX.XY, ALU.max,
                                        apply_absolute_value=True).then_inc(g_max, 1)
            gate_rounds(nc.vector, gate_max)
            dve.wait_ge(g_max, NC)
            whole(0, NC)
            dve.wait_ge(all_max, 1)
            scale(vmax[:, 0, 1:2], col(SX), 1.0 / FS, SG, KG)

            def up_max(c):
                for p in range(PR):
                    dve.wait_ge(u_done, PR * c + p + 1)
                    nc.vector.tensor_reduce(cmax[:, 1, bass.ds(PR * c + p, 1)], ps[:, p], AX.XY, ALU.max,
                                            apply_absolute_value=True).then_inc(u_max, 1)

            def gated(c, d):
                dve.wait_ge(sq_done, c + 1)
                for p in range(PR + 1):
                    if p < PR:
                        nc.vector.tensor_tensor(gb[:, c, 2 * p:2 * p + 2], ia[:, d, 2 * p:2 * p + 2],
                                                ib[:, d, 2 * p:2 * p + 2].bitcast(U16), ALU.mult).then_inc(p2_done, 1)
                    if p > 0:
                        dve.wait_ge(p2_done, PR * c + p + 2 * PR)
                        nc.vector.tensor_reduce(cmax[:, 2, bass.ds(PR * c + p - 1, 1)], gb[:, c, 2 * p - 2:2 * p], AX.XY,
                                                ALU.max, apply_absolute_value=True).then_inc(p2_max, 1)

            def both(c, d):
                up_max(c)
                gated(c - 1, d)
            up_max(0)
            rounds(nc.vector, 1, NC - 2, both)
            up_max(NC - 1)
            dve.wait_ge(u_max, PR * NC + PR)
            whole(1, PR * NC)
            gated(NC - 2, 0)
            dve.wait_ge(all_max, 2)
            scale(vmax[:, 1, 1:2], col(SX), 1.0 / FS, SU, KU)
            gated(NC - 1, 1)
            dve.wait_ge(p2_max, PR * NC)
            whole(2, PR * NC)
            dve.wait_ge(all_max, 3)
            scale(vmax[:, 2, 1:2], col(SG), 1.0 / LEVELS, S2, K2)

            def products(c, d):
                dve.wait_ge(q2_done, c + 1)
                for p in range(PR + 1):
                    if p < PR:
                        dve.wait_ge(qu_done, PR * c + p + 1 + PR)
                        nc.vector.tensor_tensor(gb[:, c, 2 * p:2 * p + 2], ia[:, d, 2 * p:2 * p + 2],
                                                ib[:, d, 2 * p:2 * p + 2], ALU.mult).then_inc(p3_done, 1)
                    if p > 0:
                        dve.wait_ge(p3_done, PR * c + p)
                        nc.vector.tensor_reduce(cmax[:, 3, bass.ds(PR * c + p - 1, 1)], gb[:, c, 2 * p - 2:2 * p], AX.XY,
                                                ALU.max, apply_absolute_value=True).then_inc(p3_max, 1)
            rounds(nc.vector, 0, NC - 1, products)
            dve.wait_ge(p3_max, PR * NC)
            whole(3, PR * NC)
            nc.vector.tensor_tensor(col(KD), col(S2), col(SU), ALU.mult).then_inc(p3_max, 1)
            dve.wait_ge(p3_max, PR * NC + 1)
            dve.wait_ge(all_max, 4)
            scale(vmax[:, 3, 1:2], col(KD), 1.0, S3, K3)
            linked(nc.vector.tensor_scalar(col(KD), col(S3), t["tgf"][:, 0:1], 1.0 / FS, ALU.mult, ALU.mult))

            def last_low(c, d):
                for b in range(CB):
                    tok = slice(b * S, (b + 1) * S)
                    dve.wait_ge(h3_done, CB * c + b + 1)
                    dve.wait_ge(d_done, CB * c + b + 1)
                    nc.vector.tensor_tensor(ia[:, d, :, tok].bitcast(F16), ib[:, d, :, tok], h3[:, d, :, tok],
                                            ALU.subtract).then_inc(l3_done, 1)

            def residual(c, d):
                for b in range(CB):
                    dve.wait_ge(y_loaded[d], 8 * (c - d) + 16)
                    dve.wait_ge(d_done, CB * c + b + 1 + 2 * CB)
                    nc.vector.scalar_tensor_tensor(out=yb[:, d, b, :], in0=ps[:, 3, b, :], scalar=col(KD),
                                                   in1=yb[:, d, b, :], op0=ALU.mult, op1=ALU.add).then_inc(z_done, 1)

            def last(c, d):
                if ahead(c, 1):
                    last_low(c + 1, 1 - d)
                residual(c, d)
            last_low(0, 0)
            rounds(nc.vector, 0, NC - 3, last)
            last(NC - 2, 0)
            last(NC - 1, 1)

        @block.gpsimd
        def _(pool):
            def over_partitions(i):
                pool.wait_ge(part_max, i + 1)
                nc.gpsimd.partition_all_reduce(vmax[:, i, 1:2], vmax[:, i, 0:1], P, RMAX).then_inc(all_max, 1)

            for i in range(4):
                over_partitions(i)

            def body(c, d):
                pool.wait_ge(z_stored[d], held(pool, 8 * CB * (c - d) + 16))
                pool.dma_start(yb[:, d], ov[bass.ds(CB * c, CB)].rearrange("b p t d -> p b (t d)")
                               ).then_inc(y_loaded[d], 16)
            rounds(nc.gpsimd, 0, NC - 1, body)

        @block.sync
        def _(sp):
            def body(c, d):
                for b in range(CB):
                    sp.wait_ge(z_done, held(sp, CB * c + b + 1 + CB))
                    sp.dma_start(ov[CB * c + b], yb[:, d, b].rearrange("p (t d) -> p t d", t=KT)
                                 ).then_inc(z_stored[d], 16)
            for d in range(2):
                sp.sem_inc(z_stored[d], 16)
            rounds(nc.sync, 0, NC - 1, body)
            for d in range(2):
                sp.wait_ge(z_stored[d], held(sp, 16 * NB // 2 + 16))


def build(nc, a, out):
    NB, S, D = out.shape
    F = a["w_gate"].shape[0]
    with ExitStack() as es:
        def sb(name, shape, dt):
            a[name] = es.enter_context(nc.sbuf_tensor(name, shape, dt))
        sb("lnall", [P, NB, S // P * D], F32)
        sb("lnmax", [P, 1], F32)
        sb("lmaxall", [P, 1], F32)
        sb("tgf", [P, 1], F32)
        sb("ident16", [P, P], F16)
        sb("wgt", [P, 2, D // P, F], F16)
        sb("wut", [P, 2, D // P, F], F16)
        sb("wdt", [P, 2, F // P, D], F16)
        attention(nc, a, a["x"], a["ctx"], out)
        feed_forward(nc, a, out)


def kernel(x, ctx_1024, g_xattn, g_ffn, L0_xattn_Wq, L0_xattn_bq, L0_xattn_Wk, L0_xattn_bk, L0_xattn_Wv, L0_xattn_bv,
           L0_xattn_Wo, L0_xattn_bo, L0_ffn_w_gate, L0_ffn_w_up, L0_ffn_w_down):
    import numpy as np
    import concourse.bacc as bacc
    from concourse.bass_utils import run_bass_kernel_spmd

    def columns(v):
        return np.asarray(v).reshape(-1, P).T

    arrays = {
        "x": x, "ctx": ctx_1024, "gx": g_xattn, "gf": g_ffn,
        "wq": np.asarray(L0_xattn_Wq).T, "wk": np.asarray(L0_xattn_Wk).T, "wv": np.asarray(L0_xattn_Wv).T,
        "wo": np.asarray(L0_xattn_Wo).T, "bq": columns(L0_xattn_bq), "bk": columns(L0_xattn_bk),
        "bv": np.asarray(L0_xattn_bv).reshape(2, 4, 2, HD).transpose(0, 2, 3, 1).reshape(4 * HD, 4), "bo": L0_xattn_bo,
        "w_gate": L0_ffn_w_gate, "w_up": L0_ffn_w_up, "w_down": L0_ffn_w_down,
    }
    nc = bacc.Bacc("TRN2", target_bir_lowering=False, num_devices=1)
    feed, aps = {}, {}
    for name, a in arrays.items():
        a = np.ascontiguousarray(a)
        feed["in_" + name] = a
        aps[name] = nc.dram_tensor("in_" + name, a.shape, mybir.dt.from_np(a.dtype), kind="ExternalInput").ap()
    out = nc.dram_tensor("out_0", x.shape, F32, kind="ExternalOutput").ap()
    build(nc, aps, out)
    r = run_bass_kernel_spmd(nc, [feed], core_ids=[0])
    return r.results[0]["out_0"]
```
